# Optimizing a Trainium2 kernel written in Bass

```python
import numpy as np
import jax
import jax.numpy as jnp

def _softmax(x, axis=-1):
    return jax.nn.softmax(x, axis=axis)

def _gelu(x):
    return jax.nn.gelu(x, approximate=True)

def _silu(x):
    return jax.nn.silu(x)

def _sigmoid(x):
    return jax.nn.sigmoid(x)

def _layernorm(x, axis=-1, eps=1e-05):
    m = jnp.mean(x, axis=axis, keepdims=True)
    v = jnp.var(x, axis=axis, keepdims=True)
    return (x - m) / jnp.sqrt(v + eps)

def _scatter_add(tgt, idx, src, axis=0):
    return tgt.at[idx].add(src)

def _segment_sum(src, seg, n):
    return jax.ops.segment_sum(src, seg, n)
kernel_name = 'mk_adj_ffn_d1_adj_r2_9b5b9e'

def setup_inputs(seed: int=0):
    np.random.seed(seed)
    _w = jnp.asarray

    def _rec_inputs():
        import jax
        import jax.numpy as jnp
        _gk = jax.random.key(seed)
        x = 7.22e-05 + 1 * jax.random.normal(jax.random.fold_in(_gk, 1), (64, 128, 256), jnp.float32)
        _a = jax.random.bernoulli(jax.random.fold_in(_gk, 2), 0.03125, (128, 128))
        _a = jnp.logical_or(_a, jnp.swapaxes(_a, -1, -2))
        _a = jnp.logical_or(_a, jnp.eye(128, dtype=bool))
        _af = _a.astype(jnp.float32)
        _af = _af * jax.random.uniform(jax.random.fold_in(_gk, 3), (128, 128), jnp.float32, 0.05, 0.00390622)
        adj = _af
        return (x, adj)
    x, adj = _rec_inputs()

    def _L0_gnn_setup():
        import jax, jax.numpy as jnp
        import numpy as np
        B, N, D, T = (64, 128, 256, 3)

        def _lin(v, W, b):
            return jnp.einsum('...i,oi->...o', v, W) + b
        key = jax.random.key(seed)
        ks = jax.random.split(key, 12)
        s2 = 1.0 / np.sqrt(2 * D)
        s1 = 1.0 / np.sqrt(D)
        return {'x': jax.random.normal(ks[0], (B, N, D), jnp.float32), 'in_mat': jax.random.uniform(ks[1], (N, N), jnp.float32) / N, 'out_mat': jax.random.uniform(ks[2], (N, N), jnp.float32) / N, 'w3_w': jax.random.normal(ks[3], (D, 2 * D), jnp.float32) * s2, 'w3_b': jnp.zeros((D,), jnp.float32), 'u3_w': jax.random.normal(ks[4], (D, D), jnp.float32) * s1, 'u3_b': jnp.zeros((D,), jnp.float32), 'w4_w': jax.random.normal(ks[5], (D, 2 * D), jnp.float32) * s2, 'w4_b': jnp.zeros((D,), jnp.float32), 'w5_w': jax.random.normal(ks[6], (D, 2 * D), jnp.float32) * s2, 'w5_b': jnp.zeros((D,), jnp.float32), 'u5_w': jax.random.normal(ks[7], (D, D), jnp.float32) * s1, 'u5_b': jnp.zeros((D,), jnp.float32)}
    _L0_gnn_all = _L0_gnn_setup()
    _L0_gnn_in = {k: v for k, v in _L0_gnn_all.items() if k in ('w3_w', 'w3_b', 'u3_w', 'u3_b', 'w4_w', 'w4_b', 'w5_w', 'w5_b', 'u5_w', 'u5_b')}
    del _L0_gnn_all

    def _L0_ffn_setup():
        import jax, jax.numpy as jnp
        import numpy as np
        D_MODEL, D_STATE, D_CONV, D_INPUT, D_OUTPUT = (512, 16, 4, 256, 256)
        EXPAND = 2
        D_INNER = EXPAND * D_MODEL
        DT_RANK = (D_MODEL + 15) // 16
        B, L = (4, 1024)

        def _mamba(x, W_in, conv_w, conv_b, W_xproj, W_dt, b_dt, A_log, Dp, W_out):
            xz = jnp.einsum('bld,ed->ble', x, W_in)
            u, z = jnp.split(xz, 2, axis=-1)
            u_pad = jnp.pad(u, ((0, 0), (D_CONV - 1, 0), (0, 0)))
            u = sum((u_pad[:, k:k + u.shape[1], :] * conv_w[:, k] for k in range(D_CONV))) + conv_b
            u = jax.nn.silu(u)
            dbc = jnp.einsum('bld,ed->ble', u, W_xproj)
            dt, B_ssm, C_ssm = jnp.split(dbc, [DT_RANK, DT_RANK + D_STATE], axis=-1)
            delta = jax.nn.softplus(jnp.einsum('blr,dr->bld', dt, W_dt) + b_dt)
            A = -jnp.exp(A_log)

            def step(h, ins):
                d_t, B_t, C_t, u_t = ins
                dA = jnp.exp(d_t[..., None] * A)
                h = dA * h + (d_t * u_t)[..., None] * B_t[:, None, :]
                y_t = jnp.einsum('bds,bs->bd', h, C_t)
                return (h, y_t)
            h0 = jnp.zeros((u.shape[0], D_INNER, D_STATE), u.dtype)
            xs = (delta.transpose(1, 0, 2), B_ssm.transpose(1, 0, 2), C_ssm.transpose(1, 0, 2), u.transpose(1, 0, 2))
            _, y = jax.lax.scan(step, h0, xs)
            y = y.transpose(1, 0, 2) + u * Dp
            y = y * jax.nn.silu(z)
            return jnp.einsum('bld,ed->ble', y, W_out)
        key = jax.random.key(seed)
        ks = jax.random.split(key, 16)
        s = lambda fan_in: 1.0 / np.sqrt(fan_in)
        inp = {'x': jax.random.normal(ks[0], (B, L, D_INPUT), jnp.float32), 'W_fc1': jax.random.normal(ks[1], (D_MODEL, D_INPUT), jnp.float32) * s(D_INPUT), 'b_fc1': jnp.zeros((D_MODEL,), jnp.float32), 'W_in': jax.random.normal(ks[2], (2 * D_INNER, D_MODEL), jnp.float32) * s(D_MODEL), 'conv_w': jax.random.normal(ks[3], (D_INNER, D_CONV), jnp.float32) * s(D_CONV), 'conv_b': jnp.zeros((D_INNER,), jnp.float32), 'W_xproj': jax.random.normal(ks[4], (DT_RANK + 2 * D_STATE, D_INNER), jnp.float32) * s(D_INNER), 'W_dt': jax.random.normal(ks[5], (D_INNER, DT_RANK), jnp.float32) * s(DT_RANK), 'b_dt': jax.random.uniform(ks[6], (D_INNER,), jnp.float32, -4.0, -2.0), 'A_log': jnp.log(jnp.broadcast_to(jnp.arange(1, D_STATE + 1, dtype=jnp.float32), (D_INNER, D_STATE))), 'D': jnp.ones((D_INNER,), jnp.float32), 'W_out': jax.random.normal(ks[7], (D_MODEL, D_INNER), jnp.float32) * s(D_INNER), 'W_fc2': jax.random.normal(ks[8], (D_OUTPUT, D_MODEL), jnp.float32) * s(D_MODEL), 'b_fc2': jnp.zeros((D_OUTPUT,), jnp.float32)}
        return inp
    _L0_ffn_all = _L0_ffn_setup()
    _L0_ffn_in = {k: v for k, v in _L0_ffn_all.items() if k in ('W_fc1', 'b_fc1', 'W_in', 'conv_w', 'conv_b', 'W_xproj', 'W_dt', 'b_dt', 'A_log', 'D', 'W_out', 'W_fc2', 'b_fc2')}
    del _L0_ffn_all
    return {'x': x, 'adj': adj, 'L0_gnn_w3_w': _L0_gnn_in['w3_w'], 'L0_gnn_w3_b': _L0_gnn_in['w3_b'], 'L0_gnn_u3_w': _L0_gnn_in['u3_w'], 'L0_gnn_u3_b': _L0_gnn_in['u3_b'], 'L0_gnn_w4_w': _L0_gnn_in['w4_w'], 'L0_gnn_w4_b': _L0_gnn_in['w4_b'], 'L0_gnn_w5_w': _L0_gnn_in['w5_w'], 'L0_gnn_w5_b': _L0_gnn_in['w5_b'], 'L0_gnn_u5_w': _L0_gnn_in['u5_w'], 'L0_gnn_u5_b': _L0_gnn_in['u5_b'], 'L0_ffn_W_fc1': _L0_ffn_in['W_fc1'], 'L0_ffn_b_fc1': _L0_ffn_in['b_fc1'], 'L0_ffn_W_in': _L0_ffn_in['W_in'], 'L0_ffn_conv_w': _L0_ffn_in['conv_w'], 'L0_ffn_conv_b': _L0_ffn_in['conv_b'], 'L0_ffn_W_xproj': _L0_ffn_in['W_xproj'], 'L0_ffn_W_dt': _L0_ffn_in['W_dt'], 'L0_ffn_b_dt': _L0_ffn_in['b_dt'], 'L0_ffn_A_log': _L0_ffn_in['A_log'], 'L0_ffn_D': _L0_ffn_in['D'], 'L0_ffn_W_out': _L0_ffn_in['W_out'], 'L0_ffn_W_fc2': _L0_ffn_in['W_fc2'], 'L0_ffn_b_fc2': _L0_ffn_in['b_fc2']}

def reference(x, adj, L0_gnn_w3_w, L0_gnn_w3_b, L0_gnn_u3_w, L0_gnn_u3_b, L0_gnn_w4_w, L0_gnn_w4_b, L0_gnn_w5_w, L0_gnn_w5_b, L0_gnn_u5_w, L0_gnn_u5_b, L0_ffn_W_fc1, L0_ffn_b_fc1, L0_ffn_W_in, L0_ffn_conv_w, L0_ffn_conv_b, L0_ffn_W_xproj, L0_ffn_W_dt, L0_ffn_b_dt, L0_ffn_A_log, L0_ffn_D, L0_ffn_W_out, L0_ffn_W_fc2, L0_ffn_b_fc2):
    import jax
    import jax.numpy as jnp

    def _L0_gnn_ref(x, in_mat, out_mat, w3_w, w3_b, u3_w, u3_b, w4_w, w4_b, w5_w, w5_b, u5_w, u5_b):
        import jax, jax.numpy as jnp
        import numpy as np
        B, N, D, T = (64, 128, 256, 3)

        def _lin(v, W, b):
            return jnp.einsum('...i,oi->...o', v, W) + b
        h = x
        for _ in range(T):
            a_in = jnp.einsum('nm,bmd->bnd', in_mat, h)
            a_out = jnp.einsum('nm,bmd->bnd', out_mat, h)
            av = jnp.concatenate([a_in, a_out], axis=-1)
            z = jax.nn.sigmoid(_lin(av, w3_w, w3_b) + _lin(h, u3_w, u3_b))
            r = jax.nn.sigmoid(_lin(av, w4_w, w4_b) + _lin(h, u3_w, u3_b))
            hv = jnp.tanh(_lin(av, w5_w, w5_b) + _lin(r * h, u5_w, u5_b))
            h = (1.0 - z) * h + z * hv
        return h

    def _L0_ffn_ref(x, W_fc1, b_fc1, W_in, conv_w, conv_b, W_xproj, W_dt, b_dt, A_log, D, W_out, W_fc2, b_fc2):
        import jax, jax.numpy as jnp
        import numpy as np
        D_MODEL, D_STATE, D_CONV, D_INPUT, D_OUTPUT = (512, 16, 4, 256, 256)
        EXPAND = 2
        D_INNER = EXPAND * D_MODEL
        DT_RANK = (D_MODEL + 15) // 16
        B, L = (4, 1024)

        def _mamba(x, W_in, conv_w, conv_b, W_xproj, W_dt, b_dt, A_log, Dp, W_out):
            xz = jnp.einsum('bld,ed->ble', x, W_in)
            u, z = jnp.split(xz, 2, axis=-1)
            u_pad = jnp.pad(u, ((0, 0), (D_CONV - 1, 0), (0, 0)))
            u = sum((u_pad[:, k:k + u.shape[1], :] * conv_w[:, k] for k in range(D_CONV))) + conv_b
            u = jax.nn.silu(u)
            dbc = jnp.einsum('bld,ed->ble', u, W_xproj)
            dt, B_ssm, C_ssm = jnp.split(dbc, [DT_RANK, DT_RANK + D_STATE], axis=-1)
            delta = jax.nn.softplus(jnp.einsum('blr,dr->bld', dt, W_dt) + b_dt)
            A = -jnp.exp(A_log)

            def step(h, ins):
                d_t, B_t, C_t, u_t = ins
                dA = jnp.exp(d_t[..., None] * A)
                h = dA * h + (d_t * u_t)[..., None] * B_t[:, None, :]
                y_t = jnp.einsum('bds,bs->bd', h, C_t)
                return (h, y_t)
            h0 = jnp.zeros((u.shape[0], D_INNER, D_STATE), u.dtype)
            xs = (delta.transpose(1, 0, 2), B_ssm.transpose(1, 0, 2), C_ssm.transpose(1, 0, 2), u.transpose(1, 0, 2))
            _, y = jax.lax.scan(step, h0, xs)
            y = y.transpose(1, 0, 2) + u * Dp
            y = y * jax.nn.silu(z)
            return jnp.einsum('bld,ed->ble', y, W_out)
        h = jnp.einsum('bli,oi->blo', x, W_fc1) + b_fc1
        h = _mamba(h, W_in, conv_w, conv_b, W_xproj, W_dt, b_dt, A_log, D, W_out)
        return jnp.einsum('bld,od->blo', h, W_fc2) + b_fc2
    x = x + _L0_gnn_ref(_layernorm(x, axis=-1), adj, adj, L0_gnn_w3_w, L0_gnn_w3_b, L0_gnn_u3_w, L0_gnn_u3_b, L0_gnn_w4_w, L0_gnn_w4_b, L0_gnn_w5_w, L0_gnn_w5_b, L0_gnn_u5_w, L0_gnn_u5_b)
    x = x + _L0_ffn_ref(_layernorm(x, axis=-1), L0_ffn_W_fc1, L0_ffn_b_fc1, L0_ffn_W_in, L0_ffn_conv_w, L0_ffn_conv_b, L0_ffn_W_xproj, L0_ffn_W_dt, L0_ffn_b_dt, L0_ffn_A_log, L0_ffn_D, L0_ffn_W_out, L0_ffn_W_fc2, L0_ffn_b_fc2)
    return x

_drawn_inputs = setup_inputs


def setup_inputs(seed=0):
    import zlib

    import numpy as np

    out = dict(_drawn_inputs(seed))
    spreads = {'L0_gnn_w3_b': (0.0, 0.435),
     'L0_gnn_u3_b': (0.0, 0.385),
     'L0_gnn_w4_b': (0.0, 0.8),
     'L0_gnn_w5_b': (0.0, 0.1),
     'L0_gnn_u5_b': (0.0, 0.1),
     'L0_ffn_b_fc1': (0.0, 0.1),
     'L0_ffn_conv_b': (0.0, 0.1),
     'L0_ffn_D': (1.0, 0.2),
     'L0_ffn_b_fc2': (0.0, 0.1)}
    factors = {'L0_gnn_w3_w': 2.818, 'L0_gnn_w4_w': 6.82}
    for name, (base, spread) in spreads.items():
        noise = np.random.default_rng([zlib.crc32(name.encode()), seed]).standard_normal(out[name].shape)
        drawn = base * np.exp(spread * noise) if base else spread * noise
        out[name] = jnp.asarray(drawn.astype(out[name].dtype))
    for name, factor in factors.items():
        out[name] = (out[name] * factor).astype(out[name].dtype)
    return out
```

```python
from collections import namedtuple
from contextlib import ExitStack

import concourse.bass as bass
from concourse import mybir

F32 = mybir.dt.float32
BF16 = mybir.dt.bfloat16
ALU = mybir.AluOpType
ACT = mybir.ActivationFunctionType

P = 128
B, L, D = 64, 128, 256
DM, DI, NS, DR = 512, 1024, 16, 32
TAPS = 4
GB = 2
G = B // GB
W = GB * L
F = D // P
M4 = DM // P
C = DI // P
Q = 4
NQ = NS // Q
STEPS = C * NQ
ROUNDS = 3
EPS = 1e-5
CAP = 30.0

GU = 2 + 5 * ROUNDS
PU_X, PU_DT, PU_B, PU_C = C, C + 1, C + 1 + C // 2, C + 1 + C // 2 + NS // 2
PU = PU_C + NS // 2

AT_T0, AT_ROUND, ROUND_STEPS = 2, 3, 8
AT_X1, AT_NORM2, AT_TX = 27, 29, 30
AT_U = 6
AT_X = AT_U + C + 2
AT_DT = AT_X + 2
AT_MIN = AT_DT + C // 2
AT_EXP, AT_MAX, AT_DU0 = AT_MIN + 1, AT_MIN + 3, AT_MIN + 4
AT_B = STEPS - NQ
AT_SAVE = 8
AT_OUT = 4

COLS = {}
_n = 0
for _name, _width in (("w3b", F), ("u3b", F), ("w4b", F), ("w5b", F), ("u5b", F), ("bfc1", M4),
                      ("convw", C * TAPS), ("convb", C), ("bdt", C), ("alog", C * NS), ("dskip", C)):
    COLS[_name] = (_n, _n + _width)
    _n += _width
NCOLS = _n

Group = namedtuple("Group", "n half par")


def stage_group(j, h, lag):
    par = (h - lag) % 2
    g = Group(2 * j + (h - lag), j + (h - lag - par) // 2, par)
    return None if isinstance(g.n, int) and not 0 <= g.n < G else g


def bodies(eng, body):
    def one(j, h):
        body(*(stage_group(j, h, lag) for lag in range(4)))
    for i in range(4):
        one(i // 2, i % 2)
    with eng.Fori(2, G // 2) as j:
        one(j, 0)
        one(j, 1)
    for i in range(G, G + 3):
        one(i // 2, i % 2)


def wait(eng, sem, value):
    if not isinstance(value, int) or value > 0:
        eng.wait_ge(sem, value)


def build(nc, x, adjT, w3T, w4T, w5T, u3T, u5T, fc1, winT, wxT, wdtT, wout, fc2T, bfc2, cols, out):
    ctx = ExitStack()
    with ctx:
        def sb(name, shape, dt=F32):
            return ctx.enter_context(nc.sbuf_tensor(name, shape, dt))

        def ps(name, shape, dt=F32):
            return ctx.enter_context(nc.psum_tensor(name, shape, dt))

        def sem(name):
            return ctx.enter_context(nc.semaphore(name))

        adj_sb = sb("adj_sb", [P, L])
        w3s = sb("w3s", [P, F, D])
        w43 = sb("w43", [P, F, D])
        w5s = sb("w5s", [P, F, D])
        u3 = sb("u3", [P, F, D])
        u5h = sb("u5h", [P, F, D])
        win = sb("win", [P, F, 2 * DI])
        wx = sb("wx", [P, C, 2 * NS + DR])
        wdt = sb("wdt", [DR, DI])
        wf = sb("wf", [P, C, D])
        sel = sb("sel", [96, 2 * NS, P], BF16)
        ident = sb("ident", [P, P])
        par = sb("par", [P, NCOLS])
        bz = sb("bz", [P, F])
        br = sb("br", [P, F])
        bv = sb("bv", [P, F])
        cu = sb("cu", [P, 2 * C])
        wcu = sb("wcu", [P, C])
        bfc2_sb = sb("bfc2_sb", [P, D])
        mhalf = sb("mhalf", [P, GB])

        xin = sb("xin", [P, 2, GB, D])
        stats = sb("stats", [P, GB, 6])
        mv = sb("mv", [P, GB, 2])
        ve = sb("ve", [P, GB])
        rstd = sb("rstd", [P, GB])
        h_tok = sb("h_tok", [P, GB, D])
        hT = sb("hT", [P, F, W])
        a_sb = sb("a_sb", [P, F, W])
        tz = sb("tz", [P, F, W])
        tr = sb("tr", [P, F, W])
        hv = sb("hv", [P, F, W])
        x1 = sb("x1", [P, GB, D])
        x1b = sb("x1b", [P, 2, GB, D])
        xnT = sb("xnT", [P, F, W])

        upad = sb("upad", [P, 2, 2, GB, TAPS - 1 + L])
        cv = sb("cv", [P, 2, 2, W])
        uth = sb("uth", [P, 2, W])
        zb = sb("zb", [P, 2, W])
        zth = sb("zth", [P, 2, W])
        u2 = sb("u2", [P, 2, C, W])
        sz2 = sb("sz2", [P, 2, C, W])
        delta = sb("delta", [P, 2, C, W])
        sp = sb("sp", [P, C, W])
        dt_sb = sb("dt_sb", [DR, W])
        rest = sb("rest", [2 * NS, W])
        mid = sb("mid", [2 * NS, W], BF16)
        split = sb("split", [96, W], BF16)
        bc = sb("bc", [P, 2, NS, W])

        du = sb("du", [P, 2, W])
        dbu = sb("dbu", [P, 2, Q, W])
        hc = sb("hc", [P, 2, Q, W])
        hs = sb("hs", [P, 2, Q, W])

        dA = ps("dA", [P, 2, Q, GB, L])
        yp = ps("yp", [P, 2, 2, W])
        gb = ps("gb", [P, 2, W])
        pb = ps("pb", [P, 2, W])

        win_raw = bc[:, :, :, :].rearrange("p a s w -> p (a s w)").rearrange("p (k e) -> p k e", k=M4)
        wout_raw = u2[:, :, :, :].rearrange("p a c w -> p (a c w)").rearrange("p (k e) -> p k e", k=M4)
        fc1_raw = dbu[:, 0, :, :]
        fc2_raw = dbu[:, 1, :, :]
        gate_raw = delta[:, :, :, :].rearrange("p a c w -> p (a c) w")

        s_load = sem("s_load")
        s_const = sem("s_const")
        s_prep = sem("s_prep")
        s_fused = sem("s_fused")
        s_kept = sem("s_kept")
        s_alog = sem("s_alog")
        x_landed = [sem("x_landed0"), sem("x_landed1")]
        out_stored = sem("out_stored")
        stats_done = sem("stats_done")
        moments = sem("moments")
        aggregated = sem("aggregated")
        rstd_done = sem("rstd_done")
        normed = sem("normed")
        gnn_mm = sem("gnn_mm")
        gnn_read = sem("gnn_read")
        rh_done = sem("rh_done")
        diff_done = sem("diff_done")
        gated = sem("gated")
        h_new = sem("h_new")
        x1_saved = sem("x1_saved")
        proj_mm = sem("proj_mm")
        proj_read = sem("proj_read")
        conv_step = sem("conv_step")
        uth_done = sem("uth_done")
        u2_done = sem("u2_done")
        zth_done = sem("zth_done")
        sz_done = sem("sz_done")
        dt_done = sem("dt_done")
        hi_done = sem("hi_done")
        mid_done = sem("mid_done")
        split_done = sem("split_done")
        sp_min = sem("sp_min")
        sp_exp = sem("sp_exp")
        sp_ln = sem("sp_ln")
        delta_done = sem("delta_done")
        du_done = sem("du_done")
        dA_done = sem("dA_done")
        dA_free = sem("dA_free")
        dbu_done = sem("dbu_done")
        scanned = sem("scanned")
        hc_even = sem("hc_even")
        hc_odd = sem("hc_odd")
        summed = sem("summed")
        y_read = sem("y_read")
        y_gated = sem("y_gated")
        out_mm = sem("out_mm")
        out_added = sem("out_added")

        block = ctx.enter_context(nc.Block())

        LOADS = [(adj_sb[:, :], adjT), (par[:, :], cols),
                 (gate_raw[:, 0:4, :], w3T.rearrange("(k p) n -> p k n", p=P)),
                 (gate_raw[:, 4:8, :], w4T.rearrange("(k p) n -> p k n", p=P)),
                 (gate_raw[:, 8:12, :], w5T.rearrange("(k p) n -> p k n", p=P)),
                 (u3[:, :, :], u3T.rearrange("(k p) n -> p k n", p=P)),
                 (u5h[:, :, :], u5T.rearrange("(k p) n -> p k n", p=P)),
                 (fc1_raw, fc1.rearrange("(k p) n -> p k n", p=P)),
                 (fc2_raw, fc2T.rearrange("(k p) n -> p k n", p=P)),
                 (wx[:, :, :], wxT.rearrange("(k p) n -> p k n", p=P)),
                 (wdt[:, :], wdtT),
                 (bfc2_sb[:, :], bfc2.partition_broadcast(P)),
                 (win_raw, winT.rearrange("(k p) n -> p k n", p=P)),
                 (wout_raw, wout.rearrange("(k p) n -> p k n", p=P))]
        N_LOAD = 16 * len(LOADS)
        N_CONST = 7
        N_PREP = 16
        N_WIN = F * (2 * DI // 512)
        N_WF = C // 2
        N_FUSED = N_WIN + N_WF + 1

        def col(name, i=0, n=1):
            a = COLS[name][0] + i
            return par[:, a:a + n]

        x_v = x.rearrange("(g b) l d -> g l b d", b=GB)
        out_v = out.rearrange("(g b) l d -> g l b d", b=GB)

        @block.sync
        def _(sp_eng):
            for dst, src in LOADS:
                sp_eng.dma_start(dst, src).then_inc(s_load, 16)

            def body(gn, pr, sc, tl):
                if gn:
                    wait(sp_eng, gnn_read, GU * gn.n - 2 * GU + GU - 1)
                    sp_eng.dma_start(xin[:, gn.par, :, :], x_v[gn.n]).then_inc(x_landed[gn.par], 16)
                if tl:
                    wait(sp_eng, out_added, tl.n + 1)
                    sp_eng.dma_start(out_v[tl.n], x1b[:, tl.par, :, :]).then_inc(out_stored, 16)

            bodies(sp_eng, body)
            sp_eng.wait_ge(out_stored, 16 * G)

        @block.tensor
        def _(pe):
            mm = nc.tensor.matmul
            banks = (gb, pb)
            pe.wait_ge(s_load, N_LOAD)
            use = 0

            def fused_bank():
                wait(pe, s_kept, use - 1)
                return banks[use % 2][:, :, :].rearrange("p a w -> p (a w)")

            for f in range(F):
                for n in range(2 * DI // 512):
                    o = fused_bank()
                    for k in range(M4):
                        last = mm(o, fc1_raw[:, k, f * P:(f + 1) * P], win_raw[:, k, n * 512:(n + 1) * 512],
                                  start=(k == 0), stop=(k == M4 - 1))
                    last.then_inc(s_fused, 1)
                    use += 1
            for n in range(N_WF):
                o = fused_bank()
                for i in range(2):
                    c = 2 * n + i
                    for k in range(M4):
                        last = mm(o[:, i * D:(i + 1) * D], wout_raw[:, k, c * P:(c + 1) * P], fc2_raw[:, k, :],
                                  start=(i == 0 and k == 0), stop=(k == M4 - 1), skip_group_check=True)
                last.then_inc(s_fused, 1)
                use += 1
            o = fused_bank()
            for e in range(2 * C):
                for k in range(M4):
                    last = mm(o[:, e:e + 1], win_raw[:, k, e * P:(e + 1) * P], col("bfc1", k),
                              start=(e == 0 and k == 0), stop=(k == M4 - 1), skip_group_check=True)
            last.then_inc(s_fused, 1)
            pe.wait_ge(s_kept, N_FUSED)
            pe.wait_ge(s_const, N_CONST)
            pe.wait_ge(s_prep, N_PREP)

            def gates(pairs, first):
                for fo in range(F):
                    for i, (w, t) in enumerate(pairs):
                        for fi in range(F):
                            last = mm(gb[:, fo, :], w[:, fi, fo * P:(fo + 1) * P], t[:, fi, :],
                                      start=(first and fo == 0 and i == 0 and fi == 0),
                                      stop=(i == len(pairs) - 1 and fi == F - 1), skip_group_check=True)
                return last

            def gnn(g, n):
                def bank(use):
                    wait(pe, gnn_read, GU * g.n + use)

                if n == AT_T0:
                    pe.wait_ge(normed, 2 * g.n + 1)
                    bank(0)
                    for b in range(GB):
                        for f in range(F):
                            last = nc.tensor.transpose(gb[:, f, b * L:(b + 1) * L],
                                                       h_tok[:, b, f * P:(f + 1) * P], ident[:, :])
                    last.then_inc(gnn_mm, 1)
                k, at = divmod(n - AT_ROUND, ROUND_STEPS)
                if 0 <= k < ROUNDS:
                    if at == 0:
                        bank(1 + 5 * k)
                        for f in range(F):
                            for b in range(GB):
                                last = mm(gb[:, f, b * L:(b + 1) * L], h_tok[:, b, f * P:(f + 1) * P],
                                          adj_sb[:, :], start=True, stop=True, skip_group_check=True)
                        last.then_inc(gnn_mm, 1)
                    if at == 1:
                        bank(2 + 5 * k)
                        gates([(w3s, a_sb), (u3, hT)], True).then_inc(gnn_mm, 1)
                    if at == 2:
                        bank(3 + 5 * k)
                        gates([(w43, a_sb)], False).then_inc(gnn_mm, 1)
                    if at == 4:
                        bank(4 + 5 * k)
                        pe.wait_ge(rh_done, ROUNDS * g.n + k + 1)
                        gates([(w5s, a_sb), (u5h, tr)], True).then_inc(gnn_mm, 1)
                    if at == 7:
                        bank(5 + 5 * k)
                        pe.wait_ge(h_new, ROUNDS * g.n + k + 1)
                        gt = gb[:, :, :].rearrange("p a w -> p (a w)")
                        for b in range(GB):
                            for f in range(F):
                                last = nc.tensor.transpose(gt[:, b * D + f * P:b * D + (f + 1) * P],
                                                           hT[:, f, b * L:(b + 1) * L], ident[:, :])
                        last.then_inc(gnn_mm, 1)
                if n == AT_TX:
                    pe.wait_ge(normed, 2 * g.n + 2)
                    bank(GU - 1)
                    for b in range(GB):
                        for f in range(F):
                            last = nc.tensor.transpose(gb[:, f, b * L:(b + 1) * L],
                                                       h_tok[:, b, f * P:(f + 1) * P], ident[:, :])
                    last.then_inc(gnn_mm, 1)

            def proj_bank(g, use):
                wait(pe, proj_read, PU * g.n + use)

            def proj(g, n):
                p, z = divmod(n - AT_U, 2)
                if 0 <= p < C // 2:
                    if n == AT_U:
                        pe.wait_ge(gnn_read, GU * g.n + GU)
                    proj_bank(g, 2 * p + z)
                    for i in range(2):
                        e = (z * C + 2 * p + i) * P
                        for f in range(F):
                            last = mm(pb[:, i, :], win[:, f, e:e + P], xnT[:, f, :],
                                      start=(i == 0 and f == 0), stop=(f == F - 1), skip_group_check=True)
                    last.then_inc(proj_mm, 1)
                if n == AT_X:
                    pe.wait_ge(u2_done, C // 2 * g.n + C // 2)
                    proj_bank(g, PU_X)
                    for c in range(C):
                        last = mm(pb[0:2 * NS + DR, 0, :], wx[:, c, :], u2[:, g.par, c, :],
                                  start=(c == 0), stop=(c == C - 1))
                    last.then_inc(proj_mm, 1)
                p = n - AT_DT
                if 0 <= p < C // 2:
                    pe.wait_ge(dt_done, g.n + 1)
                    proj_bank(g, PU_DT + p)
                    for i in range(2):
                        c = 2 * p + i
                        last = mm(pb[:, i, :], wdt[:, c * P:(c + 1) * P], dt_sb[:, :],
                                  start=(i == 0), stop=True, skip_group_check=True)
                    last.then_inc(proj_mm, 1)
                q = n - AT_B
                if q >= 0:
                    pe.wait_ge(split_done, g.n + 1)
                    spread(g, PU_B, 0, q)

            def spread(g, first, row, q):
                for r in range(Q // 2):
                    proj_bank(g, first + Q // 2 * q + r)
                    for i in range(2):
                        last = mm(pb[:, i, :], sel[:, row + Q * q + 2 * r + i, :], split[:, :],
                                  start=(i == 0), stop=True, skip_group_check=True)
                    last.then_inc(proj_mm, 1)

            def state_sum(g, m):
                c, q = divmod(m, NQ)
                if q == 0:
                    wait(pe, y_read, C * g.n + c - 1)
                    if c == 1:
                        wait(pe, out_added, g.n)
                src = hs if m % 2 else hc
                pe.wait_ge(hc_odd if m % 2 else hc_even, STEPS // 2 * g.n + m // 2 + 1)
                for s in range(Q):
                    last = mm(yp[:, c % 2, 0, :], ident[:, :], src[:, m // 2 % 2, s, :],
                              start=(q == 0 and s == 0), stop=(q == NQ - 1 and s == Q - 1))
                last.then_inc(summed, 1)

            def body(gn, pr, sc, tl):
                for n in range(STEPS):
                    if gn:
                        gnn(gn, n)
                    if sc and n < NQ:
                        spread(sc, PU_C, NS, n)
                    if pr:
                        proj(pr, n)
                    if n < 2 and tl:
                        state_sum(tl, STEPS - 2 + n)
                    if n >= 2 and sc:
                        state_sum(sc, n - 2)
                    if n == AT_OUT and tl:
                        pe.wait_ge(y_gated, C * tl.n + C)
                        for b in range(GB):
                            for c in range(C):
                                last = mm(yp[:, 1, b, :], sz2[:, tl.par, c, b * L:(b + 1) * L], wf[:, c, :],
                                          start=(b == 0 and c == 0), stop=(c == C - 1), skip_group_check=True)
                        last.then_inc(out_mm, 1)

            bodies(pe, body)

        @block.scalar
        def _(act):
            fn = nc.scalar.activation
            banks = (gb, pb)
            act.wait_ge(s_load, N_LOAD)
            fn(col("alog", 0, C * NS), col("alog", 0, C * NS), ACT.Exp).then_inc(s_alog, 1)
            use = 0
            for f in range(F):
                for n in range(2 * DI // 512):
                    act.wait_ge(s_fused, use + 1)
                    fn(win[:, f, n * 512:(n + 1) * 512], banks[use % 2][:, :, :].rearrange("p a w -> p (a w)"),
                       ACT.Copy).then_inc(s_kept, 1)
                    use += 1
            for n in range(N_WF):
                act.wait_ge(s_fused, use + 1)
                fn(wf[:, 2 * n:2 * n + 2, :], banks[use % 2][:, :, :], ACT.Copy, scale=0.25).then_inc(s_kept, 1)
                use += 1
            act.wait_ge(s_fused, use + 1)
            fn(cu[:, :], banks[use % 2][:, 0, 0:2 * C], ACT.Copy).then_inc(s_kept, 1)
            act.wait_ge(s_prep, N_PREP)
            act.wait_ge(s_const, N_CONST)

            def gnn(g, n):
                def filled(use):
                    act.wait_ge(gnn_mm, GU * g.n + use + 1)

                def gate(dst, bias, scale):
                    for fo in range(F):
                        last = fn(dst[:, fo, :], gb[:, fo, :], ACT.Tanh, bias=bias[:, fo:fo + 1], scale=scale)
                    last.then_inc(gnn_read, 1)

                if n == AT_T0:
                    filled(0)
                    fn(hT[:, :, :], gb[:, :, :], ACT.Copy).then_inc(gnn_read, 1)
                k, at = divmod(n - AT_ROUND, ROUND_STEPS)
                if 0 <= k < ROUNDS:
                    if at == 0:
                        filled(1 + 5 * k)
                        fn(a_sb[:, :, :], gb[:, :, :], ACT.Copy).then_inc(gnn_read, 1)
                    if at == 1:
                        filled(2 + 5 * k)
                        gate(tz, bz, 0.5)
                    if at == 2:
                        filled(3 + 5 * k)
                        gate(tr, br, 0.5)
                    if at == 4:
                        filled(4 + 5 * k)
                        gate(hv, bv, 1.0)
                    if at == 7 and k < ROUNDS - 1:
                        filled(5 + 5 * k)
                        fn(h_tok[:, :, :].rearrange("p b d -> p (b d)"),
                           gb[:, :, :].rearrange("p a w -> p (a w)"), ACT.Copy).then_inc(gnn_read, 1)
                if n == AT_TX:
                    filled(GU - 1)
                    fn(xnT[:, :, :], gb[:, :, :], ACT.Copy).then_inc(gnn_read, 1)

            def filled(g, use):
                act.wait_ge(proj_mm, PU * g.n + use + 1)

            def proj(g, n):
                p, odd = divmod(n - AT_U, 2)
                if 0 <= p < C // 2 and not odd:
                    s = p % 2
                    wait(act, u2_done, C // 2 * g.n + p - 1)
                    filled(g, 2 * p)
                    for i in range(2):
                        c = 2 * p + i
                        fn(upad[:, s, i, :, TAPS - 1:TAPS - 1 + L],
                           pb[:, i, :].rearrange("p (b l) -> p b l", b=GB), ACT.Identity, bias=cu[:, c:c + 1])
                        last = fn(cv[:, s, i, :], pb[:, i, :], ACT.Identity, bias=wcu[:, c:c + 1],
                                  scale=col("convw", c * TAPS + TAPS - 1))
                    last.then_inc(proj_read, 1)
                if 0 <= p < C // 2 and odd:
                    wait(act, sz_done, C // 2 * g.n + p)
                    filled(g, 2 * p + 1)
                    for i in range(2):
                        c = 2 * p + i
                        last = fn(zb[:, i, :], pb[:, i, :], ACT.Identity, bias=cu[:, C + c:C + c + 1])
                    last.then_inc(proj_read, 1)
                    act.wait_ge(proj_read, PU * g.n + 2 * p + 2)
                    fn(zth[:, :, :], zb[:, :, :], ACT.Tanh, scale=0.5).then_inc(zth_done, 1)
                p, odd = divmod(n - AT_U - 2, 2)
                if 0 <= p < C // 2 and not odd:
                    act.wait_ge(conv_step, 3 * C * g.n + 6 * p + 6)
                    wait(act, u2_done, C // 2 * g.n + p)
                    fn(uth[:, :, :], cv[:, p % 2, :, :], ACT.Tanh, scale=0.5).then_inc(uth_done, 1)
                if n == AT_X:
                    filled(g, PU_X)
                    fn(dt_sb[:, :], pb[2 * NS:2 * NS + DR, 0, :], ACT.Copy).then_inc(dt_done, 1)
                    fn(split[0:2 * NS, :], pb[0:2 * NS, 0, :], ACT.Copy).then_inc(hi_done, 1)
                if n == AT_X + 1:
                    act.wait_ge(proj_read, PU * g.n + PU_X + 1)
                    fn(split[2 * NS:4 * NS, :], rest[:, :], ACT.Copy)
                    fn(mid[:, :], rest[:, :], ACT.Copy).then_inc(mid_done, 1)
                p = n - AT_DT
                if 0 <= p < C // 2:
                    filled(g, PU_DT + p)
                    for i in range(2):
                        c = 2 * p + i
                        last = fn(delta[:, g.par, c, :], pb[:, i, :], ACT.Identity, bias=col("bdt", c))
                    last.then_inc(proj_read, 1)
                if n == AT_EXP:
                    act.wait_ge(sp_min, g.n + 1)
                    fn(sp[:, :, :], sp[:, :, :], ACT.Exp).then_inc(sp_exp, 1)
                    act.wait_ge(sp_exp, g.n + 1)
                    fn(sp[:, :, :], sp[:, :, :], ACT.Ln, bias=1.0).then_inc(sp_ln, 1)
                q = n - AT_B
                if q >= 0:
                    wait(act, dbu_done, STEPS * g.n - STEPS + AT_B + q + 1)
                    for r in range(Q // 2):
                        filled(g, PU_B + Q // 2 * q + r)
                        s = Q * q + 2 * r
                        fn(bc[:, 0, s:s + 2, :], pb[:, :, :], ACT.Copy).then_inc(proj_read, 1)

            def c_rows(g, q):
                wait(act, hc_odd if q % 2 else hc_even, STEPS // 2 * g.n - NQ // 2 + q // 2 + 1)
                for r in range(Q // 2):
                    filled(g, PU_C + Q // 2 * q + r)
                    s = Q * q + 2 * r
                    fn(bc[:, 1, s:s + 2, :], pb[:, :, :], ACT.Copy).then_inc(proj_read, 1)

            def decay(g, n):
                c, q = divmod(n, NQ)
                if n == 0:
                    act.wait_ge(delta_done, g.n + 1)
                if n % 2:
                    wait(act, scanned, STEPS * g.n + n - 1)
                else:
                    wait(act, dA_free, STEPS // 2 * g.n + n // 2)
                src = delta[:, g.par, c, :].rearrange("p (b l) -> p b l", b=GB)[:, :, 1:L]
                for i in range(Q):
                    last = fn(dA[:, n % 2, i, :, 1:L], src, ACT.Exp, scale=col("alog", c * NS + Q * q + i))
                last.then_inc(dA_done, 1)

            def body(gn, pr, sc, tl):
                for n in range(STEPS):
                    if sc and n < NQ:
                        c_rows(sc, n)
                    if sc:
                        decay(sc, n)
                    if gn:
                        gnn(gn, n)
                    if pr:
                        proj(pr, n)

            bodies(act, body)

        @block.vector
        def _(dve):
            tt = nc.vector.tensor_tensor
            stt = nc.vector.scalar_tensor_tensor
            nc.vector.memset(dA[:, :, :, :, :].rearrange("p a s b l -> p (a s b) l")[:, :, 0:1], 0.0)\
                .then_inc(s_prep, 1)
            nc.vector.memset(upad[:, :, :, :, 0:TAPS - 1].rearrange("p a i b l -> p (a i b) l"), 0.0)\
                .then_inc(s_prep, 1)
            dve.wait_ge(s_load, N_LOAD)
            for i, w in enumerate((w3s, w43, w5s)):
                raw = gate_raw[:, 4 * i:4 * i + 4, :]
                tt(w[:, :, :], raw[:, 0:F, :], raw[:, F:2 * F, :], ALU.add).then_inc(s_prep, 1)
            dve.wait_ge(s_prep, 5)
            tt(w43[:, :, :], w43[:, :, :], w3s[:, :, :], ALU.subtract).then_inc(s_prep, 1)
            nc.vector.tensor_scalar(u5h[:, :, :], u5h[:, :, :], 0.5, None, ALU.mult).then_inc(s_prep, 1)
            nc.vector.tensor_scalar(wx[:, :, :], wx[:, :, :], 0.5, None, ALU.mult).then_inc(s_prep, 1)
            tt(bz[:, :], col("w3b", 0, F), col("u3b", 0, F), ALU.add).then_inc(s_prep, 1)
            tt(br[:, :], col("w4b", 0, F), col("u3b", 0, F), ALU.add).then_inc(s_prep, 1)
            tt(bv[:, :], col("w5b", 0, F), col("u5b", 0, F), ALU.add).then_inc(s_prep, 1)
            dve.wait_ge(s_prep, 11)
            nc.vector.tensor_scalar(bz[:, :], bz[:, :], 0.5, None, ALU.mult).then_inc(s_prep, 1)
            nc.vector.tensor_scalar(br[:, :], br[:, :], 0.5, None, ALU.mult).then_inc(s_prep, 1)
            dve.wait_ge(s_alog, 1)
            nc.vector.tensor_scalar(col("alog", 0, C * NS), col("alog", 0, C * NS), -1.0, None, ALU.mult)\
                .then_inc(s_prep, 1)
            dve.wait_ge(s_kept, N_FUSED)
            last_tap = col("convw", 0, C * TAPS).rearrange("p (c t) -> p c t", t=TAPS)[:, :, TAPS - 1]
            tt(wcu[:, :], last_tap, cu[:, 0:C], ALU.mult).then_inc(s_prep, 1)
            dve.wait_ge(s_prep, N_PREP - 1)
            tt(wcu[:, :], wcu[:, :], col("convb", 0, C), ALU.add).then_inc(s_prep, 1)
            dve.wait_ge(s_prep, N_PREP)

            def norm_stats(src, done):
                for b in range(GB):
                    last = nc.vector.bn_stats(stats[:, b, :], src[:, b, :])
                last.then_inc(stats_done, 1)
                dve.wait_ge(stats_done, done)
                nc.vector.memset(ve[:, :], 0.0)
                for b in range(GB):
                    last = nc.vector.bn_aggr(mv[:, b, :], stats[:, b, :])
                last.then_inc(aggregated, 1)
                dve.wait_ge(aggregated, done)
                nc.vector.tensor_scalar(ve[:, :], mv[:, :, 1], EPS, None, ALU.add).then_inc(moments, 1)

            def normalise(dst, src):
                for b in range(GB):
                    last = nc.vector.tensor_scalar(dst[:, b, :], src[:, b, :], mv[:, b, 0:1], rstd[:, b:b + 1],
                                                   ALU.subtract, ALU.mult)
                last.then_inc(normed, 1)

            def gnn(g, n):
                if n == 0:
                    dve.wait_ge(x_landed[g.par], 16 * g.half + 16)
                    norm_stats(xin[:, g.par, :, :], 2 * g.n + 1)
                if n == 1:
                    dve.wait_ge(rstd_done, 2 * g.n + 1)
                    wait(dve, gnn_read, GU * g.n)
                    normalise(h_tok, xin[:, g.par, :, :])
                k, at = divmod(n - AT_ROUND, ROUND_STEPS)
                if 0 <= k < ROUNDS:
                    if at == 3:
                        dve.wait_ge(gnn_read, GU * g.n + 4 + 5 * k)
                        stt(tr[:, :, :], tr[:, :, :], 1.0, hT[:, :, :], ALU.add, ALU.mult).then_inc(rh_done, 1)
                    if at == 5:
                        dve.wait_ge(diff_done, ROUNDS * g.n + k + 1)
                        stt(hv[:, :, :], tz[:, :, :], 1.0, hv[:, :, :], ALU.add, ALU.mult).then_inc(gated, 1)
                    if at == 6:
                        dve.wait_ge(gated, ROUNDS * g.n + k + 1)
                        stt(hT[:, :, :], hv[:, :, :], 0.5, hT[:, :, :], ALU.mult, ALU.add).then_inc(h_new, 1)
                if n == AT_X1:
                    dve.wait_ge(gnn_mm, GU * g.n + GU - 1)
                    wait(dve, x1_saved, g.n)
                    tt(x1[:, :, :].rearrange("p b d -> p (b d)"), gb[:, :, :].rearrange("p a w -> p (a w)"),
                       xin[:, g.par, :, :].rearrange("p b d -> p (b d)"), ALU.add).then_inc(gnn_read, 1)
                    dve.wait_ge(gnn_read, GU * g.n + GU - 1)
                    norm_stats(x1, 2 * g.n + 2)
                if n == AT_NORM2:
                    dve.wait_ge(rstd_done, 2 * g.n + 2)
                    normalise(h_tok, x1)

            def proj(g, n):
                p, odd = divmod(n - AT_U - 1, 2)
                if 0 <= p < C // 2 and not odd:
                    s = p % 2
                    dve.wait_ge(proj_read, PU * g.n + 2 * p + 1)
                    for k in range(TAPS - 1):
                        for i in range(2):
                            c = 2 * p + i
                            if k:
                                dve.wait_ge(conv_step, 3 * C * g.n + 6 * p + 2 * k - 1 + i)
                            acc = cv[:, s, i, :].rearrange("p (b l) -> p b l", b=GB)
                            stt(acc, upad[:, s, i, :, k:k + L], col("convw", c * TAPS + k), acc,
                                ALU.mult, ALU.add).then_inc(conv_step, 1)
                p, odd = divmod(n - AT_U - 2, 2)
                if 0 <= p < C // 2 and not odd:
                    dve.wait_ge(zth_done, C // 2 * g.n + p + 1)
                    if p == 0:
                        wait(dve, out_mm, g.n - 1)
                    stt(sz2[:, g.par, 2 * p:2 * p + 2, :], zth[:, :, :], 1.0, zb[:, :, :], ALU.add, ALU.mult)\
                        .then_inc(sz_done, 1)
                if 0 <= p < C // 2 and odd:
                    dve.wait_ge(uth_done, C // 2 * g.n + p + 1)
                    stt(u2[:, g.par, 2 * p:2 * p + 2, :], uth[:, :, :], 1.0, cv[:, p % 2, :, :],
                        ALU.add, ALU.mult).then_inc(u2_done, 1)
                if n == AT_X + 1:
                    dve.wait_ge(hi_done, g.n + 1)
                    tt(rest[:, :], pb[0:2 * NS, 0, :], split[0:2 * NS, :], ALU.subtract).then_inc(proj_read, 1)
                if n == AT_X + 2:
                    dve.wait_ge(mid_done, g.n + 1)
                    tt(split[4 * NS:6 * NS, :], rest[:, :], mid[:, :], ALU.subtract).then_inc(split_done, 1)
                if n == AT_MIN:
                    dve.wait_ge(proj_read, PU * g.n + PU_B)
                    nc.vector.tensor_scalar(sp[:, :, :], delta[:, g.par, :, :], CAP, None, ALU.min)\
                        .then_inc(sp_min, 1)
                if n == AT_MAX:
                    dve.wait_ge(sp_ln, g.n + 1)
                    tt(delta[:, g.par, :, :], delta[:, g.par, :, :], sp[:, :, :], ALU.max).then_inc(delta_done, 1)
                if n == AT_DU0:
                    dve.wait_ge(delta_done, g.n + 1)
                    wait(dve, dbu_done, STEPS * g.n - NQ)
                    input_scale(g, 0)

            def input_scale(g, c):
                tt(du[:, c % 2, :], delta[:, g.par, c, :], u2[:, g.par, c, :], ALU.mult).then_inc(du_done, 1)

            def scan(g, n):
                dve.wait_ge(dA_done, STEPS * g.n + n + 1)
                dve.wait_ge(dbu_done, STEPS * g.n + n + 1)
                a = dA[:, n % 2, :, :, :].rearrange("p s b l -> p (s b l)")
                if n % 2:
                    wait(dve, summed, STEPS * g.n + n - 3)
                    dst = hs[:, n // 2 % 2, :, :].rearrange("p s w -> p (s w)")
                else:
                    dst = a
                nc.vector.tensor_tensor_scan(dst, a, dbu[:, n % 2, :, :].rearrange("p s w -> p (s w)"),
                                             0.0, ALU.mult, ALU.add).then_inc(scanned, 1)

            def times_c(g, n):
                c, q = divmod(n, NQ)
                dve.wait_ge(scanned, STEPS * g.n + n + 1)
                if c == 0:
                    dve.wait_ge(proj_read, PU * g.n + PU_C + Q // 2 * (q + 1))
                wait(dve, summed, STEPS * g.n + n - 3)
                tt(hc[:, n // 2 % 2, :, :].rearrange("p s w -> p (s w)"),
                   dA[:, 0, :, :, :].rearrange("p s b l -> p (s b l)"),
                   bc[:, 1, Q * q:Q * q + Q, :].rearrange("p s w -> p (s w)"), ALU.mult).then_inc(hc_even, 1)

            def first_zeros(g, n):
                dve.wait_ge(hc_even, STEPS // 2 * g.n + n // 2 + 1)
                nc.vector.memset(dA[:, 0, :, :, :].rearrange("p s b l -> p (s b) l")[:, :, 0:1], 0.0)\
                    .then_inc(dA_free, 1)

            def gate_y(g, c):
                dve.wait_ge(summed, STEPS * g.n + NQ * (c + 1))
                y = u2[:, g.par, c, :]
                stt(y, y, col("dskip", c), yp[:, c % 2, 0, :], ALU.mult, ALU.add)\
                    .then_inc(y_read, 1)
                dve.wait_ge(y_read, C * g.n + c + 1)
                tt(sz2[:, g.par, c, :], y, sz2[:, g.par, c, :], ALU.mult).then_inc(y_gated, 1)

            def body(gn, pr, sc, tl):
                for n in range(STEPS):
                    if sc:
                        scan(sc, n)
                        if n % NQ == 1 and n // NQ < C - 1:
                            c = n // NQ + 1
                            if c >= 2:
                                dve.wait_ge(dbu_done, STEPS * sc.n + NQ * (c - 1))
                            input_scale(sc, c)
                    if gn:
                        gnn(gn, n)
                    if sc and n % 2:
                        times_c(sc, n - 1)
                    if sc and n >= 7 and n % NQ == 3:
                        gate_y(sc, (n - 7) // NQ)
                    if tl and n == 3:
                        gate_y(tl, C - 1)
                    if pr:
                        proj(pr, n)
                    if tl and n == AT_OUT + 1:
                        dve.wait_ge(out_mm, tl.n + 1)
                        dve.wait_ge(x1_saved, tl.n + 1)
                        res = x1b[:, tl.par, :, :]
                        tt(res, yp[:, 1, :, :], res, ALU.add).then_inc(out_added, 1)
                    if sc and n % 2:
                        first_zeros(sc, n - 1)

            bodies(dve, body)

        @block.gpsimd
        def _(pool):
            tt = nc.gpsimd.tensor_tensor
            nc.gpsimd.memset(ident[:, :], 0.0).then_inc(s_const, 1)
            nc.gpsimd.memset(sel[:, :, :], 0.0).then_inc(s_const, 1)
            nc.gpsimd.memset(mhalf[:, :], -0.5).then_inc(s_const, 1)
            pool.wait_ge(s_const, 3)
            nc.gpsimd.affine_select(out=ident[:, :], in_=ident[:, :], compare_op=ALU.not_equal, fill=1.0,
                                    base=0, pattern=[[-1, P]], channel_multiplier=1).then_inc(s_const, 1)
            for part in range(3):
                nc.gpsimd.affine_select(out=sel[:, :, :], in_=sel[:, :, :], compare_op=ALU.not_equal, fill=1.0,
                                        base=-2 * NS * part, pattern=[[-1, 2 * NS], [0, P]],
                                        channel_multiplier=1).then_inc(s_const, 1)
                pool.wait_ge(s_const, 5 + part)
            pool.wait_ge(s_load, N_LOAD)
            pool.wait_ge(s_prep, N_PREP)
            pool.wait_ge(s_kept, N_FUSED)

            def rstd_of(done):
                pool.wait_ge(moments, done)
                tt(rstd[:, :], ve[:, :], mhalf[:, :], ALU.pow).then_inc(rstd_done, 1)

            def gnn(g, n):
                if n == 0:
                    rstd_of(2 * g.n + 1)
                k, at = divmod(n - AT_ROUND, ROUND_STEPS)
                if 0 <= k < ROUNDS and at == 4:
                    pool.wait_ge(gnn_read, GU * g.n + 5 + 5 * k)
                    tt(hv[:, :, :], hv[:, :, :], hT[:, :, :], ALU.subtract).then_inc(diff_done, 1)
                if n == AT_X1:
                    rstd_of(2 * g.n + 2)

            def input_rows(g, n):
                c, q = divmod(n, NQ)
                if q == 0:
                    pool.wait_ge(du_done, C * g.n + c + 1)
                if c == 0:
                    pool.wait_ge(proj_read, PU * g.n + PU_B + Q // 2 * (q + 1))
                wait(pool, scanned, STEPS * g.n + n - 1)
                tt(dbu[:, n % 2, :, :], du[:, c % 2, :].unsqueeze(1).to_broadcast([P, Q, W]),
                   bc[:, 0, Q * q:Q * q + Q, :], ALU.mult).then_inc(dbu_done, 1)

            def times_c(g, n):
                c, q = divmod(n, NQ)
                pool.wait_ge(scanned, STEPS * g.n + n + 1)
                if c == 0:
                    pool.wait_ge(proj_read, PU * g.n + PU_C + Q // 2 * (q + 1))
                h = hs[:, n // 2 % 2, :, :]
                tt(h, h, bc[:, 1, Q * q:Q * q + Q, :], ALU.mult).then_inc(hc_odd, 1)

            def body(gn, pr, sc, tl):
                for n in range(STEPS):
                    if sc:
                        input_rows(sc, n)
                    if tl and n == 0:
                        times_c(tl, STEPS - 1)
                    if sc and n and n % 2 == 0:
                        times_c(sc, n - 1)
                    if gn:
                        gnn(gn, n)
                    if pr and n == AT_SAVE:
                        pool.wait_ge(gnn_read, GU * pr.n + GU - 1)
                        wait(pool, out_stored, 16 * pr.n - 16)
                        tt(x1b[:, pr.par, :, :], x1[:, :, :],
                           bfc2_sb[:, :].unsqueeze(1).to_broadcast([P, GB, D]), ALU.add).then_inc(x1_saved, 1)

            bodies(pool, body)


def kernel(**inputs):
    import numpy as np
    import concourse.bacc as bacc
    from concourse.bass_utils import run_bass_kernel_spmd

    def get(name):
        return np.asarray(inputs[name])

    def column(v):
        v = v.reshape(v.shape[0] // P, P, -1)
        return v.transpose(1, 0, 2).reshape(P, -1)

    f = "L0_ffn_"
    n = "L0_gnn_"
    cols = np.concatenate([column(get(k)) for k in (
        n + "w3_b", n + "u3_b", n + "w4_b", n + "w5_b", n + "u5_b", f + "b_fc1", f + "conv_w",
        f + "conv_b", f + "b_dt", f + "A_log", f + "D")], axis=1)
    wxp = get(f + "W_xproj")
    arrays = {
        "x": get("x"), "adjT": get("adj").T,
        "w3T": get(n + "w3_w").T, "w4T": get(n + "w4_w").T, "w5T": get(n + "w5_w").T,
        "u3T": get(n + "u3_w").T, "u5T": get(n + "u5_w").T,
        "fc1": get(f + "W_fc1"), "winT": get(f + "W_in").T,
        "wxT": np.concatenate([wxp[DR:], wxp[:DR]], axis=0).T, "wdtT": get(f + "W_dt").T,
        "wout": get(f + "W_out"), "fc2T": get(f + "W_fc2").T, "bfc2": get(f + "b_fc2"), "cols": cols,
    }
    arrays = {k: np.ascontiguousarray(v) for k, v in arrays.items()}
    nc = bacc.Bacc("TRN2", target_bir_lowering=False, num_devices=1)
    args = [nc.dram_tensor(f"in_{k}", v.shape, mybir.dt.from_np(v.dtype), kind="ExternalInput").ap()
            for k, v in arrays.items()]
    args.append(nc.dram_tensor("out_0", (B, L, D), F32, kind="ExternalOutput").ap())
    build(nc, *args)
    r = run_bass_kernel_spmd(nc, [{f"in_{k}": v for k, v in arrays.items()}], core_ids=[0])
    return r.results[0]["out_0"]
```

```python
from collections import namedtuple
from contextlib import ExitStack

import concourse.bass as bass
from concourse import mybir

F32 = mybir.dt.float32
BF16 = mybir.dt.bfloat16
ALU = mybir.AluOpType
ACT = mybir.ActivationFunctionType

P = 128
B, L, D = 64, 128, 256
DM, DI, NS, DR = 512, 1024, 16, 32
TAPS = 4
GB = 2
G = B // GB
W = GB * L
F = D // P
M4 = DM // P
C = DI // P
Q = 4
NQ = NS // Q
STEPS = C * NQ
ROUNDS = 3
EPS = 1e-5
CAP = 30.0

GU = 2 + 5 * ROUNDS

AT_T0, AT_ROUND, ROUND_STEPS = 2, 3, 9
AT_A, AT_ZG, AT_RG, AT_HV, AT_T = 0, 1, 3, 4, 8
AT_X1 = AT_ROUND + ROUNDS * ROUND_STEPS
AT_U = (6, 8, 10, 12)
AT_Z = (9, 11, 24, 26)
AT_X = 18
AT_DT = (19, 20, 21, 22)
AT_MIN, AT_EXP, AT_MAX, AT_DU0 = 24, 25, 27, 28
AT_C = STEPS - 1
AT_B = AT_C - NQ
AT_SAVE = 8
AT_GATE7, AT_OUT, AT_ADD = 2, 3, 6
OUT_PARTS = 3

PROJ_ORDER = sorted(AT_U + AT_Z + (AT_X,) + AT_DT)
PU_U, PU_Z, PU_DT = ([PROJ_ORDER.index(n) for n in at] for at in (AT_U, AT_Z, AT_DT))
PU_X = PROJ_ORDER.index(AT_X)
PU_B = len(PROJ_ORDER)
PU_C = PU_B + NS // 2
PU = PU_C + NS // 2

COLS = {}
_n = 0
for _name, _width in (("w3b", F), ("u3b", F), ("w4b", F), ("w5b", F), ("u5b", F), ("bfc1", M4),
                      ("convw", C * TAPS), ("convb", C), ("bdt", C), ("alog", C * NS), ("dskip", C)):
    COLS[_name] = (_n, _n + _width)
    _n += _width
NCOLS = _n

Group = namedtuple("Group", "n half par")


def stage_group(j, h, lag):
    par = (h - lag) % 2
    g = Group(2 * j + (h - lag), j + (h - lag - par) // 2, par)
    return None if isinstance(g.n, int) and not 0 <= g.n < G else g


def bodies(eng, body):
    def one(j, h):
        body(*(stage_group(j, h, lag) for lag in range(4)))
    for i in range(4):
        one(i // 2, i % 2)
    with eng.Fori(2, G // 2) as j:
        one(j, 0)
        one(j, 1)
    for i in range(G, G + 3):
        one(i // 2, i % 2)


def wait(eng, sem, value):
    if not isinstance(value, int) or value > 0:
        eng.wait_ge(sem, value)


def build(nc, x, adjT, w3T, w4T, w5T, u3T, u5T, fc1, winT, wxT, wdtT, wout, fc2T, bfc2, cols, out):
    ctx = ExitStack()
    with ctx:
        def sb(name, shape, dt=F32):
            return ctx.enter_context(nc.sbuf_tensor(name, shape, dt))

        def ps(name, shape, dt=F32):
            return ctx.enter_context(nc.psum_tensor(name, shape, dt))

        def sem(name):
            return ctx.enter_context(nc.semaphore(name))

        adj_sb = sb("adj_sb", [P, L])
        w3s = sb("w3s", [P, F, D])
        w43 = sb("w43", [P, F, D])
        w5s = sb("w5s", [P, F, D])
        u3 = sb("u3", [P, F, D])
        u5h = sb("u5h", [P, F, D])
        win = sb("win", [P, F, 2 * DI])
        wx = sb("wx", [P, C, 2 * NS + DR])
        wdt = sb("wdt", [DR, DI])
        wf = sb("wf", [P, C, D])
        sel = sb("sel", [96, 2 * NS, P], BF16)
        ident = sb("ident", [P, P])
        par = sb("par", [P, NCOLS])
        bz = sb("bz", [P, F])
        br = sb("br", [P, F])
        bv = sb("bv", [P, F])
        cu = sb("cu", [P, 2 * C])
        wcu = sb("wcu", [P, C])
        bfc2_sb = sb("bfc2_sb", [P, D])
        mhalf = sb("mhalf", [P, GB])

        xin = sb("xin", [P, 2, GB, D])
        stats = sb("stats", [P, GB, 6])
        mv = sb("mv", [P, GB, 2])
        ve = sb("ve", [P, GB])
        rstd = sb("rstd", [P, GB])
        h_tok = sb("h_tok", [P, GB, D])
        hT = sb("hT", [P, F, W])
        a_sb = sb("a_sb", [P, F, W])
        tz = sb("tz", [P, F, W])
        tr = sb("tr", [P, F, W])
        hv = sb("hv", [P, F, W])
        x1 = sb("x1", [P, GB, D])
        x1b = sb("x1b", [P, 2, GB, D])
        xnT = sb("xnT", [P, F, W])

        upad = sb("upad", [P, 2, 2, GB, TAPS - 1 + L])
        cv = sb("cv", [P, 2, 2, W])
        uth = sb("uth", [P, 2, W])
        zb = sb("zb", [P, 2, W])
        zth = sb("zth", [P, 2, W])
        u2 = sb("u2", [P, 2, C, W])
        sz2 = sb("sz2", [P, 2, C, W])
        delta = sb("delta", [P, 2, C, W])
        sp = sb("sp", [P, C, W])
        dt_sb = sb("dt_sb", [DR, W])
        rest = sb("rest", [2 * NS, W])
        mid = sb("mid", [2 * NS, W], BF16)
        split = sb("split", [96, W], BF16)
        bc = sb("bc", [P, 2, NS, W])

        du = sb("du", [P, 2, W])
        dbu = sb("dbu", [P, 2, Q, W])
        hc = sb("hc", [P, 2, Q, W])
        hs = sb("hs", [P, 2, Q, W])

        dA = ps("dA", [P, 2, Q, GB, L])
        yp = ps("yp", [P, 2, 2, W])
        gb = ps("gb", [P, 2, W])
        pb = ps("pb", [P, 2, W])

        win_raw = bc[:, :, :, :].rearrange("p a s w -> p (a s w)").rearrange("p (k e) -> p k e", k=M4)
        wout_raw = u2[:, :, :, :].rearrange("p a c w -> p (a c w)").rearrange("p (k e) -> p k e", k=M4)
        fc1_raw = dbu[:, 0, :, :]
        fc2_raw = dbu[:, 1, :, :]
        gate_raw = delta[:, :, :, :].rearrange("p a c w -> p (a c) w")

        s_load = sem("s_load")
        s_const = sem("s_const")
        s_prep = sem("s_prep")
        s_fused = sem("s_fused")
        s_kept = sem("s_kept")
        s_alog = sem("s_alog")
        x_landed = [sem("x_landed0"), sem("x_landed1")]
        out_stored = sem("out_stored")
        stats_done = sem("stats_done")
        moments = sem("moments")
        aggregated = sem("aggregated")
        rstd_done = sem("rstd_done")
        normed = sem("normed")
        gnn_mm = sem("gnn_mm")
        gnn_read = sem("gnn_read")
        rh_done = sem("rh_done")
        diff_done = sem("diff_done")
        gated = sem("gated")
        h_new = sem("h_new")
        x1_saved = sem("x1_saved")
        proj_mm = sem("proj_mm")
        proj_read = sem("proj_read")
        conv_step = sem("conv_step")
        uth_done = sem("uth_done")
        u2_done = sem("u2_done")
        zth_done = sem("zth_done")
        sz_done = sem("sz_done")
        dt_done = sem("dt_done")
        hi_done = sem("hi_done")
        mid_done = sem("mid_done")
        split_done = sem("split_done")
        sp_min = sem("sp_min")
        sp_exp = sem("sp_exp")
        sp_ln = sem("sp_ln")
        delta_done = sem("delta_done")
        du_done = sem("du_done")
        dA_done = sem("dA_done")
        dA_free = sem("dA_free")
        dbu_done = sem("dbu_done")
        scanned = sem("scanned")
        hc_even = sem("hc_even")
        hc_odd = sem("hc_odd")
        summed = sem("summed")
        y_read = sem("y_read")
        y_gated = sem("y_gated")
        out_mm = sem("out_mm")
        out_added = sem("out_added")

        block = ctx.enter_context(nc.Block())

        LOADS = [(adj_sb[:, :], adjT), (par[:, :], cols),
                 (gate_raw[:, 0:4, :], w3T.rearrange("(k p) n -> p k n", p=P)),
                 (gate_raw[:, 4:8, :], w4T.rearrange("(k p) n -> p k n", p=P)),
                 (gate_raw[:, 8:12, :], w5T.rearrange("(k p) n -> p k n", p=P)),
                 (u3[:, :, :], u3T.rearrange("(k p) n -> p k n", p=P)),
                 (u5h[:, :, :], u5T.rearrange("(k p) n -> p k n", p=P)),
                 (fc1_raw, fc1.rearrange("(k p) n -> p k n", p=P)),
                 (fc2_raw, fc2T.rearrange("(k p) n -> p k n", p=P)),
                 (wx[:, :, :], wxT.rearrange("(k p) n -> p k n", p=P)),
                 (wdt[:, :], wdtT),
                 (bfc2_sb[:, :], bfc2.partition_broadcast(P)),
                 (win_raw, winT.rearrange("(k p) n -> p k n", p=P)),
                 (wout_raw, wout.rearrange("(k p) n -> p k n", p=P))]
        N_LOAD = 16 * len(LOADS)
        N_CONST = 7
        N_PREP = 16
        N_WIN = F * (2 * DI // 512)
        N_WF = C // 2
        N_FUSED = N_WIN + N_WF + 1

        def col(name, i=0, n=1):
            a = COLS[name][0] + i
            return par[:, a:a + n]

        x_v = x.rearrange("(g b) l d -> g l b d", b=GB)
        out_v = out.rearrange("(g b) l d -> g l b d", b=GB)

        @block.sync
        def _(sp_eng):
            for dst, src in LOADS:
                sp_eng.dma_start(dst, src).then_inc(s_load, 16)

            def body(gn, pr, sc, tl):
                if gn:
                    wait(sp_eng, gnn_read, GU * gn.n - 2 * GU + GU - 1)
                    sp_eng.dma_start(xin[:, gn.par, :, :], x_v[gn.n]).then_inc(x_landed[gn.par], 16)
                if tl:
                    wait(sp_eng, out_added, tl.n + 1)
                    sp_eng.dma_start(out_v[tl.n], x1b[:, tl.par, :, :]).then_inc(out_stored, 16)

            bodies(sp_eng, body)
            sp_eng.wait_ge(out_stored, 16 * G)

        @block.tensor
        def _(pe):
            mm = nc.tensor.matmul
            banks = (gb, pb)
            pe.wait_ge(s_load, N_LOAD)
            use = 0

            def fused_bank():
                wait(pe, s_kept, use - 1)
                return banks[use % 2][:, :, :].rearrange("p a w -> p (a w)")

            for f in range(F):
                for n in range(2 * DI // 512):
                    o = fused_bank()
                    for k in range(M4):
                        last = mm(o, fc1_raw[:, k, f * P:(f + 1) * P], win_raw[:, k, n * 512:(n + 1) * 512],
                                  start=(k == 0), stop=(k == M4 - 1))
                    last.then_inc(s_fused, 1)
                    use += 1
            for n in range(N_WF):
                o = fused_bank()
                for i in range(2):
                    c = 2 * n + i
                    for k in range(M4):
                        last = mm(o[:, i * D:(i + 1) * D], wout_raw[:, k, c * P:(c + 1) * P], fc2_raw[:, k, :],
                                  start=(i == 0 and k == 0), stop=(k == M4 - 1), skip_group_check=True)
                last.then_inc(s_fused, 1)
                use += 1
            o = fused_bank()
            for e in range(2 * C):
                for k in range(M4):
                    last = mm(o[:, e:e + 1], win_raw[:, k, e * P:(e + 1) * P], col("bfc1", k),
                              start=(e == 0 and k == 0), stop=(k == M4 - 1), skip_group_check=True)
            last.then_inc(s_fused, 1)
            pe.wait_ge(s_kept, N_FUSED)
            pe.wait_ge(s_const, N_CONST)
            pe.wait_ge(s_prep, N_PREP)

            def gates(pairs, first, final=True):
                for fo in range(F):
                    for i, (w, t) in enumerate(pairs):
                        for fi in range(F):
                            last = mm(gb[:, fo, :], w[:, fi, fo * P:(fo + 1) * P], t[:, fi, :],
                                      start=(first and fo == 0 and i == 0 and fi == 0),
                                      stop=(final and i == len(pairs) - 1 and fi == F - 1), skip_group_check=True)
                return last

            def gnn(g, n):
                def bank(use):
                    wait(pe, gnn_read, GU * g.n + use)

                if n == AT_T0:
                    pe.wait_ge(normed, 2 * g.n + 1)
                    bank(0)
                    for b in range(GB):
                        for f in range(F):
                            last = nc.tensor.transpose(gb[:, f, b * L:(b + 1) * L],
                                                       h_tok[:, b, f * P:(f + 1) * P], ident[:, :])
                    last.then_inc(gnn_mm, 1)
                k, at = divmod(n - AT_ROUND, ROUND_STEPS)
                if 0 <= k < ROUNDS:
                    if at == AT_A:
                        bank(1 + 5 * k)
                        for f in range(F):
                            for b in range(GB):
                                last = mm(gb[:, f, b * L:(b + 1) * L], h_tok[:, b, f * P:(f + 1) * P],
                                          adj_sb[:, :], start=True, stop=True, skip_group_check=True)
                        last.then_inc(gnn_mm, 1)
                    if at == AT_ZG:
                        bank(2 + 5 * k)
                        gates([(w3s, a_sb)], True, False)
                    if at == AT_ZG + 1:
                        gates([(u3, hT)], False).then_inc(gnn_mm, 1)
                    if at == AT_RG:
                        bank(3 + 5 * k)
                        gates([(w43, a_sb)], False).then_inc(gnn_mm, 1)
                    if at == AT_HV:
                        bank(4 + 5 * k)
                        gates([(w5s, a_sb)], True, False)
                    if at == AT_HV + 1:
                        pe.wait_ge(rh_done, ROUNDS * g.n + k + 1)
                        gates([(u5h, tr)], False).then_inc(gnn_mm, 1)
                    if at == AT_T:
                        bank(5 + 5 * k)
                        pe.wait_ge(h_new, ROUNDS * g.n + k + 1)
                        gt = gb[:, :, :].rearrange("p a w -> p (a w)")
                        for b in range(GB):
                            for f in range(F):
                                last = nc.tensor.transpose(gt[:, b * D + f * P:b * D + (f + 1) * P],
                                                           hT[:, f, b * L:(b + 1) * L], ident[:, :])
                        last.then_inc(gnn_mm, 1)

            def norm2_turned(g):
                pe.wait_ge(normed, 2 * g.n + 2)
                pe.wait_ge(gnn_read, GU * g.n + GU - 1)
                for b in range(GB):
                    for f in range(F):
                        last = nc.tensor.transpose(gb[:, f, b * L:(b + 1) * L],
                                                   h_tok[:, b, f * P:(f + 1) * P], ident[:, :])
                last.then_inc(gnn_mm, 1)

            def proj_bank(g, use):
                wait(pe, proj_read, PU * g.n + use)

            def proj(g, n):
                if n in AT_U or n in AT_Z:
                    if n == AT_U[0]:
                        pe.wait_ge(gnn_read, GU * g.n + GU)
                    proj_bank(g, PROJ_ORDER.index(n))
                    first = 2 * AT_U.index(n) if n in AT_U else C + 2 * AT_Z.index(n)
                    for i in range(2):
                        e = (first + i) * P
                        for f in range(F):
                            last = mm(pb[:, i, :], win[:, f, e:e + P], xnT[:, f, :],
                                      start=(i == 0 and f == 0), stop=(f == F - 1), skip_group_check=True)
                    last.then_inc(proj_mm, 1)
                if n == AT_X:
                    pe.wait_ge(u2_done, C // 2 * g.n + C // 2)
                    proj_bank(g, PU_X)
                    for c in range(C):
                        last = mm(pb[0:2 * NS + DR, 0, :], wx[:, c, :], u2[:, g.par, c, :],
                                  start=(c == 0), stop=(c == C - 1))
                    last.then_inc(proj_mm, 1)
                if n in AT_DT:
                    pe.wait_ge(dt_done, g.n + 1)
                    p = AT_DT.index(n)
                    proj_bank(g, PU_DT[p])
                    for i in range(2):
                        c = 2 * p + i
                        last = mm(pb[:, i, :], wdt[:, c * P:(c + 1) * P], dt_sb[:, :],
                                  start=(i == 0), stop=True, skip_group_check=True)
                    last.then_inc(proj_mm, 1)

            def spread(g, first, row, q, r):
                proj_bank(g, first + Q // 2 * q + r)
                for i in range(2):
                    last = mm(pb[:, i, :], sel[:, row + Q * q + 2 * r + i, :], split[:, :],
                              start=(i == 0), stop=True, skip_group_check=True)
                last.then_inc(proj_mm, 1)

            def rows(sc, pr, n, r):
                if pr and AT_B <= n < AT_C:
                    if n == AT_B and r == 0:
                        pe.wait_ge(split_done, pr.n + 1)
                    spread(pr, PU_B, 0, n - AT_B, r)
                if pr and n == AT_C:
                    spread(pr, PU_C, NS, 0, r)
                if sc and n < NQ - 1:
                    spread(sc, PU_C, NS, n + 1, r)

            def state_sum(g, m):
                c, q = divmod(m, NQ)
                if q == 0:
                    wait(pe, y_read, C * g.n + c - 1)
                    if c == 1:
                        wait(pe, out_added, g.n)
                src = hs if m % 2 else hc
                pe.wait_ge(hc_odd if m % 2 else hc_even, STEPS // 2 * g.n + m // 2 + 1)
                for s in range(Q):
                    last = mm(yp[:, c % 2, 0, :], ident[:, :], src[:, m // 2 % 2, s, :],
                              start=(q == 0 and s == 0), stop=(q == NQ - 1 and s == Q - 1))
                last.then_inc(summed, 1)

            def out_part(g, part):
                if part == 0:
                    pe.wait_ge(y_gated, C * g.n + C)
                todo = [(b, c) for b in range(GB) for c in range(C)]
                for b, c in todo[part * len(todo) // OUT_PARTS:(part + 1) * len(todo) // OUT_PARTS]:
                    last = mm(yp[:, 1, b, :], sz2[:, g.par, c, b * L:(b + 1) * L], wf[:, c, :],
                              start=(b == 0 and c == 0), stop=(c == C - 1), skip_group_check=True)
                if part == OUT_PARTS - 1:
                    last.then_inc(out_mm, 1)

            def body(gn, pr, sc, tl):
                for n in range(STEPS):
                    rows(sc, pr, n, 0)
                    if n < 2 and tl:
                        state_sum(tl, STEPS - 2 + n)
                    if n >= 2 and sc:
                        state_sum(sc, n - 2)
                    rows(sc, pr, n, 1)
                    if pr and n == 0:
                        norm2_turned(pr)
                    if gn:
                        gnn(gn, n)
                    if pr:
                        proj(pr, n)
                    if tl and AT_OUT <= n < AT_OUT + OUT_PARTS:
                        out_part(tl, n - AT_OUT)

            bodies(pe, body)

        @block.scalar
        def _(act):
            fn = nc.scalar.activation
            banks = (gb, pb)
            act.wait_ge(s_load, N_LOAD)
            fn(col("alog", 0, C * NS), col("alog", 0, C * NS), ACT.Exp).then_inc(s_alog, 1)
            use = 0
            for f in range(F):
                for n in range(2 * DI // 512):
                    act.wait_ge(s_fused, use + 1)
                    fn(win[:, f, n * 512:(n + 1) * 512], banks[use % 2][:, :, :].rearrange("p a w -> p (a w)"),
                       ACT.Copy).then_inc(s_kept, 1)
                    use += 1
            for n in range(N_WF):
                act.wait_ge(s_fused, use + 1)
                fn(wf[:, 2 * n:2 * n + 2, :], banks[use % 2][:, :, :], ACT.Copy, scale=0.25).then_inc(s_kept, 1)
                use += 1
            act.wait_ge(s_fused, use + 1)
            fn(cu[:, :], banks[use % 2][:, 0, 0:2 * C], ACT.Copy).then_inc(s_kept, 1)
            act.wait_ge(s_prep, N_PREP)
            act.wait_ge(s_const, N_CONST)

            def gnn(g, n):
                def filled(use):
                    act.wait_ge(gnn_mm, GU * g.n + use + 1)

                def gate(dst, bias, scale):
                    for fo in range(F):
                        last = fn(dst[:, fo, :], gb[:, fo, :], ACT.Tanh, bias=bias[:, fo:fo + 1], scale=scale)
                    last.then_inc(gnn_read, 1)

                if n == AT_T0:
                    filled(0)
                    fn(hT[:, :, :], gb[:, :, :], ACT.Copy).then_inc(gnn_read, 1)
                k, at = divmod(n - AT_ROUND, ROUND_STEPS)
                if 0 <= k < ROUNDS:
                    if at == AT_A:
                        filled(1 + 5 * k)
                        fn(a_sb[:, :, :], gb[:, :, :], ACT.Copy).then_inc(gnn_read, 1)
                    if at == AT_ZG + 1:
                        filled(2 + 5 * k)
                        gate(tz, bz, 0.5)
                    if at == AT_RG:
                        filled(3 + 5 * k)
                        gate(tr, br, 0.5)
                    if at == AT_HV + 1:
                        filled(4 + 5 * k)
                        gate(hv, bv, 1.0)
                    if at == AT_T and k < ROUNDS - 1:
                        filled(5 + 5 * k)
                        fn(h_tok[:, :, :].rearrange("p b d -> p (b d)"),
                           gb[:, :, :].rearrange("p a w -> p (a w)"), ACT.Copy).then_inc(gnn_read, 1)

            def norm2_kept(g):
                act.wait_ge(gnn_mm, GU * g.n + GU)
                fn(xnT[:, :, :], gb[:, :, :], ACT.Copy).then_inc(gnn_read, 1)

            def filled(g, use):
                act.wait_ge(proj_mm, PU * g.n + use + 1)

            def proj(g, n):
                if n - 1 in AT_U:
                    p = AT_U.index(n - 1)
                    s = p % 2
                    wait(act, u2_done, C // 2 * g.n + p - 1)
                    filled(g, PU_U[p])
                    for i in range(2):
                        c = 2 * p + i
                        fn(upad[:, s, i, :, TAPS - 1:TAPS - 1 + L],
                           pb[:, i, :].rearrange("p (b l) -> p b l", b=GB), ACT.Identity, bias=cu[:, c:c + 1])
                        last = fn(cv[:, s, i, :], pb[:, i, :], ACT.Identity, bias=wcu[:, c:c + 1],
                                  scale=col("convw", c * TAPS + TAPS - 1))
                    last.then_inc(proj_read, 1)
                if n - 1 in AT_Z:
                    p = AT_Z.index(n - 1)
                    wait(act, sz_done, C // 2 * g.n + p)
                    filled(g, PU_Z[p])
                    for i in range(2):
                        c = 2 * p + i
                        last = fn(zb[:, i, :], pb[:, i, :], ACT.Identity, bias=cu[:, C + c:C + c + 1])
                    last.then_inc(proj_read, 1)
                    act.wait_ge(proj_read, PU * g.n + PU_Z[p] + 1)
                    fn(zth[:, :, :], zb[:, :, :], ACT.Tanh, scale=0.5).then_inc(zth_done, 1)
                if n - 3 in AT_U:
                    p = AT_U.index(n - 3)
                    act.wait_ge(conv_step, 3 * C * g.n + 6 * p + 6)
                    wait(act, u2_done, C // 2 * g.n + p)
                    fn(uth[:, :, :], cv[:, p % 2, :, :], ACT.Tanh, scale=0.5).then_inc(uth_done, 1)
                if n == AT_X + 1:
                    filled(g, PU_X)
                    fn(dt_sb[:, :], pb[2 * NS:2 * NS + DR, 0, :], ACT.Copy).then_inc(dt_done, 1)
                    fn(split[0:2 * NS, :], pb[0:2 * NS, 0, :], ACT.Copy).then_inc(hi_done, 1)
                if n == AT_X + 2:
                    act.wait_ge(proj_read, PU * g.n + PU_X + 1)
                    fn(split[2 * NS:4 * NS, :], rest[:, :], ACT.Copy)
                    fn(mid[:, :], rest[:, :], ACT.Copy).then_inc(mid_done, 1)
                if n - 1 in AT_DT:
                    p = AT_DT.index(n - 1)
                    filled(g, PU_DT[p])
                    for i in range(2):
                        c = 2 * p + i
                        last = fn(delta[:, g.par, c, :], pb[:, i, :], ACT.Identity, bias=col("bdt", c))
                    last.then_inc(proj_read, 1)
                if n == AT_EXP:
                    act.wait_ge(sp_min, g.n + 1)
                    fn(sp[:, :, :], sp[:, :, :], ACT.Exp).then_inc(sp_exp, 1)
                    act.wait_ge(sp_exp, g.n + 1)
                    fn(sp[:, :, :], sp[:, :, :], ACT.Ln, bias=1.0).then_inc(sp_ln, 1)

            def rows(sc, pr, n, r):
                if pr and AT_B <= n < AT_C:
                    q = n - AT_B
                    if r == 0:
                        wait(act, dbu_done, STEPS * pr.n - NQ + q + 1)
                    keep(pr, PU_B, 0, q, r)
                if pr and n == AT_C:
                    c_rows(pr, 0, r)
                if sc and n < NQ - 1:
                    c_rows(sc, n + 1, r)

            def c_rows(g, q, r):
                if r == 0:
                    wait(act, hc_odd if q % 2 else hc_even, STEPS // 2 * g.n - NQ // 2 + q // 2 + 1)
                keep(g, PU_C, 1, q, r)

            def keep(g, first, which, q, r):
                filled(g, first + Q // 2 * q + r)
                s = Q * q + 2 * r
                fn(bc[:, which, s:s + 2, :], pb[:, :, :], ACT.Copy).then_inc(proj_read, 1)

            def decay(g, n):
                c, q = divmod(n, NQ)
                if n == 0:
                    act.wait_ge(delta_done, g.n + 1)
                if n % 2:
                    wait(act, scanned, STEPS * g.n + n - 1)
                else:
                    wait(act, dA_free, STEPS // 2 * g.n + n // 2)
                src = delta[:, g.par, c, :].rearrange("p (b l) -> p b l", b=GB)[:, :, 1:L]
                for i in range(Q):
                    last = fn(dA[:, n % 2, i, :, 1:L], src, ACT.Exp, scale=col("alog", c * NS + Q * q + i))
                last.then_inc(dA_done, 1)

            def body(gn, pr, sc, tl):
                for n in range(STEPS):
                    if n:
                        rows(sc, pr, n - 1, 1)
                    elif sc:
                        c_rows(sc, 0, 1)
                    if sc and n < STEPS - 1:
                        decay(sc, n + 1)
                    if pr and n == STEPS - 1:
                        decay(pr, 0)
                    if pr and n == 1:
                        norm2_kept(pr)
                    if gn and n:
                        gnn(gn, n - 1)
                    if pr:
                        proj(pr, n)
                    rows(sc, pr, n, 0)

            bodies(act, body)

        @block.vector
        def _(dve):
            tt = nc.vector.tensor_tensor
            stt = nc.vector.scalar_tensor_tensor
            nc.vector.memset(dA[:, :, :, :, :].rearrange("p a s b l -> p (a s b) l")[:, :, 0:1], 0.0)\
                .then_inc(s_prep, 1)
            nc.vector.memset(upad[:, :, :, :, 0:TAPS - 1].rearrange("p a i b l -> p (a i b) l"), 0.0)\
                .then_inc(s_prep, 1)
            dve.wait_ge(s_load, N_LOAD)
            for i, w in enumerate((w3s, w43, w5s)):
                raw = gate_raw[:, 4 * i:4 * i + 4, :]
                tt(w[:, :, :], raw[:, 0:F, :], raw[:, F:2 * F, :], ALU.add).then_inc(s_prep, 1)
            dve.wait_ge(s_prep, 5)
            tt(w43[:, :, :], w43[:, :, :], w3s[:, :, :], ALU.subtract).then_inc(s_prep, 1)
            nc.vector.tensor_scalar(u5h[:, :, :], u5h[:, :, :], 0.5, None, ALU.mult).then_inc(s_prep, 1)
            nc.vector.tensor_scalar(wx[:, :, :], wx[:, :, :], 0.5, None, ALU.mult).then_inc(s_prep, 1)
            tt(bz[:, :], col("w3b", 0, F), col("u3b", 0, F), ALU.add).then_inc(s_prep, 1)
            tt(br[:, :], col("w4b", 0, F), col("u3b", 0, F), ALU.add).then_inc(s_prep, 1)
            tt(bv[:, :], col("w5b", 0, F), col("u5b", 0, F), ALU.add).then_inc(s_prep, 1)
            dve.wait_ge(s_prep, 11)
            nc.vector.tensor_scalar(bz[:, :], bz[:, :], 0.5, None, ALU.mult).then_inc(s_prep, 1)
            nc.vector.tensor_scalar(br[:, :], br[:, :], 0.5, None, ALU.mult).then_inc(s_prep, 1)
            dve.wait_ge(s_alog, 1)
            nc.vector.tensor_scalar(col("alog", 0, C * NS), col("alog", 0, C * NS), -1.0, None, ALU.mult)\
                .then_inc(s_prep, 1)
            dve.wait_ge(s_kept, N_FUSED)
            last_tap = col("convw", 0, C * TAPS).rearrange("p (c t) -> p c t", t=TAPS)[:, :, TAPS - 1]
            tt(wcu[:, :], last_tap, cu[:, 0:C], ALU.mult).then_inc(s_prep, 1)
            dve.wait_ge(s_prep, N_PREP - 1)
            tt(wcu[:, :], wcu[:, :], col("convb", 0, C), ALU.add).then_inc(s_prep, 1)
            dve.wait_ge(s_prep, N_PREP)

            def norm_stats(src, done):
                for b in range(GB):
                    last = nc.vector.bn_stats(stats[:, b, :], src[:, b, :])
                last.then_inc(stats_done, 1)
                dve.wait_ge(stats_done, done)
                nc.vector.memset(ve[:, :], 0.0)
                for b in range(GB):
                    last = nc.vector.bn_aggr(mv[:, b, :], stats[:, b, :])
                last.then_inc(aggregated, 1)
                dve.wait_ge(aggregated, done)
                nc.vector.tensor_scalar(ve[:, :], mv[:, :, 1], EPS, None, ALU.add).then_inc(moments, 1)

            def normalise(dst, src):
                for b in range(GB):
                    last = nc.vector.tensor_scalar(dst[:, b, :], src[:, b, :], mv[:, b, 0:1], rstd[:, b:b + 1],
                                                   ALU.subtract, ALU.mult)
                last.then_inc(normed, 1)

            def gnn(g, n):
                if n == 0:
                    dve.wait_ge(x_landed[g.par], 16 * g.half + 16)
                    norm_stats(xin[:, g.par, :, :], 2 * g.n + 1)
                if n == AT_T0:
                    dve.wait_ge(rstd_done, 2 * g.n + 1)
                    wait(dve, gnn_read, GU * g.n)
                    normalise(h_tok, xin[:, g.par, :, :])
                k, at = divmod(n - AT_ROUND, ROUND_STEPS)
                if 0 <= k < ROUNDS:
                    if at == AT_HV + 1:
                        dve.wait_ge(gnn_read, GU * g.n + 4 + 5 * k)
                        stt(tr[:, :, :], tr[:, :, :], 1.0, hT[:, :, :], ALU.add, ALU.mult).then_inc(rh_done, 1)
                    if at == AT_T:
                        dve.wait_ge(diff_done, ROUNDS * g.n + k + 1)
                        stt(hv[:, :, :], tz[:, :, :], 1.0, hv[:, :, :], ALU.add, ALU.mult).then_inc(gated, 1)
                        dve.wait_ge(gated, ROUNDS * g.n + k + 1)
                        stt(hT[:, :, :], hv[:, :, :], 0.5, hT[:, :, :], ALU.mult, ALU.add).then_inc(h_new, 1)
                if n == AT_X1:
                    dve.wait_ge(gnn_mm, GU * g.n + GU - 1)
                    wait(dve, x1_saved, g.n)
                    tt(x1[:, :, :].rearrange("p b d -> p (b d)"), gb[:, :, :].rearrange("p a w -> p (a w)"),
                       xin[:, g.par, :, :].rearrange("p b d -> p (b d)"), ALU.add).then_inc(gnn_read, 1)
                    dve.wait_ge(gnn_read, GU * g.n + GU - 1)
                    norm_stats(x1, 2 * g.n + 2)

            def proj(g, n):
                if n - 2 in AT_U:
                    p = AT_U.index(n - 2)
                    s = p % 2
                    dve.wait_ge(proj_read, PU * g.n + PU_U[p] + 1)
                    for k in range(TAPS - 1):
                        for i in range(2):
                            c = 2 * p + i
                            if k:
                                dve.wait_ge(conv_step, 3 * C * g.n + 6 * p + 2 * k - 1 + i)
                            acc = cv[:, s, i, :].rearrange("p (b l) -> p b l", b=GB)
                            stt(acc, upad[:, s, i, :, k:k + L], col("convw", c * TAPS + k), acc,
                                ALU.mult, ALU.add).then_inc(conv_step, 1)
                if n - 2 in AT_Z:
                    p = AT_Z.index(n - 2)
                    dve.wait_ge(zth_done, C // 2 * g.n + p + 1)
                    if p == 0:
                        wait(dve, out_mm, g.n - 1)
                    stt(sz2[:, g.par, 2 * p:2 * p + 2, :], zth[:, :, :], 1.0, zb[:, :, :], ALU.add, ALU.mult)\
                        .then_inc(sz_done, 1)
                if n - 4 in AT_U:
                    p = AT_U.index(n - 4)
                    dve.wait_ge(uth_done, C // 2 * g.n + p + 1)
                    stt(u2[:, g.par, 2 * p:2 * p + 2, :], uth[:, :, :], 1.0, cv[:, p % 2, :, :],
                        ALU.add, ALU.mult).then_inc(u2_done, 1)
                if n == AT_X + 2:
                    dve.wait_ge(hi_done, g.n + 1)
                    tt(rest[:, :], pb[0:2 * NS, 0, :], split[0:2 * NS, :], ALU.subtract).then_inc(proj_read, 1)
                if n == AT_X + 3:
                    dve.wait_ge(mid_done, g.n + 1)
                    tt(split[4 * NS:6 * NS, :], rest[:, :], mid[:, :], ALU.subtract).then_inc(split_done, 1)
                if n == AT_MIN:
                    dve.wait_ge(proj_read, PU * g.n + PU_DT[-1] + 1)
                    nc.vector.tensor_scalar(sp[:, :, :], delta[:, g.par, :, :], CAP, None, ALU.min)\
                        .then_inc(sp_min, 1)
                if n == AT_MAX:
                    dve.wait_ge(sp_ln, g.n + 1)
                    tt(delta[:, g.par, :, :], delta[:, g.par, :, :], sp[:, :, :], ALU.max).then_inc(delta_done, 1)
                if n == AT_DU0:
                    dve.wait_ge(delta_done, g.n + 1)
                    wait(dve, dbu_done, STEPS * g.n - NQ)
                    input_scale(g, 0)

            def input_scale(g, c):
                tt(du[:, c % 2, :], delta[:, g.par, c, :], u2[:, g.par, c, :], ALU.mult).then_inc(du_done, 1)

            def scan(g, n):
                dve.wait_ge(dA_done, STEPS * g.n + n + 1)
                dve.wait_ge(dbu_done, STEPS * g.n + n + 1)
                a = dA[:, n % 2, :, :, :].rearrange("p s b l -> p (s b l)")
                if n % 2:
                    wait(dve, summed, STEPS * g.n + n - 3)
                    dst = hs[:, n // 2 % 2, :, :].rearrange("p s w -> p (s w)")
                else:
                    dst = a
                nc.vector.tensor_tensor_scan(dst, a, dbu[:, n % 2, :, :].rearrange("p s w -> p (s w)"),
                                             0.0, ALU.mult, ALU.add).then_inc(scanned, 1)

            def times_c(g, n):
                c, q = divmod(n, NQ)
                dve.wait_ge(scanned, STEPS * g.n + n + 1)
                if c == 0:
                    dve.wait_ge(proj_read, PU * g.n + PU_C + Q // 2 * (q + 1))
                wait(dve, summed, STEPS * g.n + n - 3)
                tt(hc[:, n // 2 % 2, :, :].rearrange("p s w -> p (s w)"),
                   dA[:, 0, :, :, :].rearrange("p s b l -> p (s b l)"),
                   bc[:, 1, Q * q:Q * q + Q, :].rearrange("p s w -> p (s w)"), ALU.mult).then_inc(hc_even, 1)

            def first_zeros(g, n):
                dve.wait_ge(hc_even, STEPS // 2 * g.n + n // 2 + 1)
                nc.vector.memset(dA[:, 0, :, :, :].rearrange("p s b l -> p (s b) l")[:, :, 0:1], 0.0)\
                    .then_inc(dA_free, 1)

            def gate_y(g, c):
                dve.wait_ge(summed, STEPS * g.n + NQ * (c + 1))
                y = u2[:, g.par, c, :]
                stt(y, y, col("dskip", c), yp[:, c % 2, 0, :], ALU.mult, ALU.add)\
                    .then_inc(y_read, 1)
                dve.wait_ge(y_read, C * g.n + c + 1)
                tt(sz2[:, g.par, c, :], y, sz2[:, g.par, c, :], ALU.mult).then_inc(y_gated, 1)

            def body(gn, pr, sc, tl):
                for n in range(STEPS):
                    if sc:
                        scan(sc, n)
                    if pr and n == 0:
                        dve.wait_ge(rstd_done, 2 * pr.n + 2)
                        normalise(h_tok, x1)
                    if gn:
                        gnn(gn, n)
                    if sc and n % 2 == 0:
                        times_c(sc, n)
                    if sc and n % NQ == 1 and n // NQ < C - 1:
                        c = n // NQ + 1
                        if c >= 2:
                            dve.wait_ge(dbu_done, STEPS * sc.n + NQ * (c - 1))
                        input_scale(sc, c)
                    if sc and n >= NQ + 3 and n % NQ == 3:
                        gate_y(sc, n // NQ - 1)
                    if tl and n == AT_GATE7:
                        gate_y(tl, C - 1)
                    if tl and n == AT_ADD:
                        dve.wait_ge(out_mm, tl.n + 1)
                        dve.wait_ge(x1_saved, tl.n + 1)
                        res = x1b[:, tl.par, :, :]
                        tt(res, yp[:, 1, :, :], res, ALU.add).then_inc(out_added, 1)
                    if sc and n % 2 == 0:
                        first_zeros(sc, n)
                    if pr:
                        proj(pr, n)

            bodies(dve, body)

        @block.gpsimd
        def _(pool):
            tt = nc.gpsimd.tensor_tensor
            nc.gpsimd.memset(ident[:, :], 0.0).then_inc(s_const, 1)
            nc.gpsimd.memset(sel[:, :, :], 0.0).then_inc(s_const, 1)
            nc.gpsimd.memset(mhalf[:, :], -0.5).then_inc(s_const, 1)
            pool.wait_ge(s_const, 3)
            nc.gpsimd.affine_select(out=ident[:, :], in_=ident[:, :], compare_op=ALU.not_equal, fill=1.0,
                                    base=0, pattern=[[-1, P]], channel_multiplier=1).then_inc(s_const, 1)
            for part in range(3):
                nc.gpsimd.affine_select(out=sel[:, :, :], in_=sel[:, :, :], compare_op=ALU.not_equal, fill=1.0,
                                        base=-2 * NS * part, pattern=[[-1, 2 * NS], [0, P]],
                                        channel_multiplier=1).then_inc(s_const, 1)
                pool.wait_ge(s_const, 5 + part)
            pool.wait_ge(s_load, N_LOAD)
            pool.wait_ge(s_prep, N_PREP)
            pool.wait_ge(s_kept, N_FUSED)

            def rstd_of(done):
                pool.wait_ge(moments, done)
                tt(rstd[:, :], ve[:, :], mhalf[:, :], ALU.pow).then_inc(rstd_done, 1)

            def gnn(g, n):
                if n == 1:
                    rstd_of(2 * g.n + 1)
                k, at = divmod(n - AT_ROUND, ROUND_STEPS)
                if 0 <= k < ROUNDS and at == AT_HV + 3:
                    pool.wait_ge(gnn_read, GU * g.n + 5 + 5 * k)
                    tt(hv[:, :, :], hv[:, :, :], hT[:, :, :], ALU.subtract).then_inc(diff_done, 1)
                if n == AT_X1 + 1:
                    rstd_of(2 * g.n + 2)

            def input_rows(g, n):
                c, q = divmod(n, NQ)
                if q == 0:
                    pool.wait_ge(du_done, C * g.n + c + 1)
                if c == 0:
                    pool.wait_ge(proj_read, PU * g.n + PU_B + Q // 2 * (q + 1))
                wait(pool, scanned, STEPS * g.n + n - 1)
                tt(dbu[:, n % 2, :, :], du[:, c % 2, :].unsqueeze(1).to_broadcast([P, Q, W]),
                   bc[:, 0, Q * q:Q * q + Q, :], ALU.mult).then_inc(dbu_done, 1)

            def times_c(g, n):
                c, q = divmod(n, NQ)
                pool.wait_ge(scanned, STEPS * g.n + n + 1)
                if c == 0:
                    pool.wait_ge(proj_read, PU * g.n + PU_C + Q // 2 * (q + 1))
                h = hs[:, n // 2 % 2, :, :]
                tt(h, h, bc[:, 1, Q * q:Q * q + Q, :], ALU.mult).then_inc(hc_odd, 1)

            def body(gn, pr, sc, tl):
                for n in range(STEPS):
                    if sc and n < STEPS - 1:
                        input_rows(sc, n + 1)
                    if pr and n == STEPS - 1:
                        input_rows(pr, 0)
                    if tl and n == 0:
                        times_c(tl, STEPS - 1)
                    if sc and n and n % 2 == 0:
                        times_c(sc, n - 1)
                    if gn:
                        gnn(gn, n)
                    if pr and n == AT_SAVE:
                        pool.wait_ge(gnn_read, GU * pr.n + GU - 1)
                        wait(pool, out_stored, 16 * pr.n - 16)
                        tt(x1b[:, pr.par, :, :], x1[:, :, :],
                           bfc2_sb[:, :].unsqueeze(1).to_broadcast([P, GB, D]), ALU.add).then_inc(x1_saved, 1)

            bodies(pool, body)


def kernel(**inputs):
    import numpy as np
    import concourse.bacc as bacc
    from concourse.bass_utils import run_bass_kernel_spmd

    def get(name):
        return np.asarray(inputs[name])

    def column(v):
        v = v.reshape(v.shape[0] // P, P, -1)
        return v.transpose(1, 0, 2).reshape(P, -1)

    f = "L0_ffn_"
    n = "L0_gnn_"
    cols = np.concatenate([column(get(k)) for k in (
        n + "w3_b", n + "u3_b", n + "w4_b", n + "w5_b", n + "u5_b", f + "b_fc1", f + "conv_w",
        f + "conv_b", f + "b_dt", f + "A_log", f + "D")], axis=1)
    wxp = get(f + "W_xproj")
    arrays = {
        "x": get("x"), "adjT": get("adj").T,
        "w3T": get(n + "w3_w").T, "w4T": get(n + "w4_w").T, "w5T": get(n + "w5_w").T,
        "u3T": get(n + "u3_w").T, "u5T": get(n + "u5_w").T,
        "fc1": get(f + "W_fc1"), "winT": get(f + "W_in").T,
        "wxT": np.concatenate([wxp[DR:], wxp[:DR]], axis=0).T, "wdtT": get(f + "W_dt").T,
        "wout": get(f + "W_out"), "fc2T": get(f + "W_fc2").T, "bfc2": get(f + "b_fc2"), "cols": cols,
    }
    arrays = {k: np.ascontiguousarray(v) for k, v in arrays.items()}
    nc = bacc.Bacc("TRN2", target_bir_lowering=False, num_devices=1)
    args = [nc.dram_tensor(f"in_{k}", v.shape, mybir.dt.from_np(v.dtype), kind="ExternalInput").ap()
            for k, v in arrays.items()]
    args.append(nc.dram_tensor("out_0", (B, L, D), F32, kind="ExternalOutput").ap())
    build(nc, *args)
    r = run_bass_kernel_spmd(nc, [{f"in_{k}": v for k, v in arrays.items()}], core_ids=[0])
    return r.results[0]["out_0"]
```

```python
from collections import namedtuple
from contextlib import ExitStack

import concourse.bass as bass
from concourse import mybir

F32 = mybir.dt.float32
BF16 = mybir.dt.bfloat16
ALU = mybir.AluOpType
ACT = mybir.ActivationFunctionType

P = 128
B, L, D = 64, 128, 256
DM, DI, NS, DR = 512, 1024, 16, 32
TAPS = 4
GB = 2
G = B // GB
W = GB * L
F = D // P
M4 = DM // P
C = DI // P
Q = 4
NQ = NS // Q
STEPS = C * NQ
ROUNDS = 3
EPS = 1e-5
CAP = 30.0

GU = 2 + 5 * ROUNDS

AT_T0, AT_ROUND, ROUND_STEPS = 2, 3, 9
AT_A, AT_ZG, AT_RG, AT_HV, AT_RH, AT_DIFF, AT_T = 0, (1, 2), 3, (4, 5), 4, 7, 8
AT_X1 = AT_ROUND + ROUNDS * ROUND_STEPS
AT_U = (3, 6, 9, 12)
AT_Z = (11, 15, 24, 26)
AT_X = (16, 17)
AT_DT = (19, 20, 21, 22)
AT_MIN, AT_EXP, AT_LN, AT_MAX, AT_DU0 = 23, 24, 26, (27, 28), 29
AT_C = STEPS - 1
AT_B = AT_C - NQ
AT_SAVE = 14
AT_GATE7 = 2
AT_OUT = tuple(range(2, 2 + 2 * NQ))
AT_ADD = (7, 12)

PROJ_ORDER = sorted(AT_U + AT_Z + AT_X[:1] + AT_DT)
PU_U, PU_Z, PU_DT = ([PROJ_ORDER.index(n) for n in at] for at in (AT_U, AT_Z, AT_DT))
PU_X = PROJ_ORDER.index(AT_X[0])
PU_B = len(PROJ_ORDER)
PU_C = PU_B + NS // 2
PU = PU_C + NS // 2

COLS = {}
_n = 0
for _name, _width in (("w3b", F), ("u3b", F), ("w4b", F), ("w5b", F), ("u5b", F), ("bfc1", M4),
                      ("convw", C * TAPS), ("convb", C), ("bdt", C), ("alog", C * NS), ("dskip", C)):
    COLS[_name] = (_n, _n + _width)
    _n += _width
NCOLS = _n

Group = namedtuple("Group", "n half par")


def stage_group(j, h, lag):
    par = (h - lag) % 2
    g = Group(2 * j + (h - lag), j + (h - lag - par) // 2, par)
    return None if isinstance(g.n, int) and not 0 <= g.n < G else g


def bodies(eng, body):
    def one(j, h, **kind):
        body(*(stage_group(j, h, lag) for lag in range(4)), **kind)
    one(0, 0, fuse=True)
    for i in range(1, 4):
        one(i // 2, i % 2)
    with eng.Fori(2, G // 2) as j:
        one(j, 0)
        one(j, 1)
    for i in range(G, G + 3):
        one(i // 2, i % 2)


def wait(eng, sem, value):
    if not isinstance(value, int) or value > 0:
        eng.wait_ge(sem, value)


def build(nc, x, adjT, w3T, w4T, w5T, u3T, u5T, fc1, winT, wxT, wdtT, wout, fc2T, bfc2, cols, out):
    ctx = ExitStack()
    with ctx:
        def sb(name, shape, dt=F32):
            return ctx.enter_context(nc.sbuf_tensor(name, shape, dt))

        def ps(name, shape, dt=F32):
            return ctx.enter_context(nc.psum_tensor(name, shape, dt))

        def sem(name):
            return ctx.enter_context(nc.semaphore(name))

        adj_sb = sb("adj_sb", [P, L])
        w3s = sb("w3s", [P, F, D])
        w43 = sb("w43", [P, F, D])
        w5s = sb("w5s", [P, F, D])
        u3 = sb("u3", [P, F, D])
        u5h = sb("u5h", [P, F, D])
        win = sb("win", [P, F, 2 * DI])
        wx = sb("wx", [P, C, 2 * NS + DR])
        wdt = sb("wdt", [DR, DI])
        wf = sb("wf", [P, C, D])
        sel = sb("sel", [96, 2 * NS, P], BF16)
        ident = sb("ident", [P, P])
        par = sb("par", [P, NCOLS])
        bz = sb("bz", [P, F])
        br = sb("br", [P, F])
        bv = sb("bv", [P, F])
        cu = sb("cu", [P, 2 * C])
        wcu = sb("wcu", [P, C])
        bfc2_sb = sb("bfc2_sb", [P, D])
        mhalf = sb("mhalf", [P, GB])

        xin = sb("xin", [P, 2, GB, D])
        stats = sb("stats", [P, GB, 6])
        mv = sb("mv", [P, GB, 2])
        ve = sb("ve", [P, GB])
        rstd = sb("rstd", [P, GB])
        h_tok = sb("h_tok", [P, GB, D])
        hT = sb("hT", [P, F, W])
        a_sb = sb("a_sb", [P, F, W])
        tz = sb("tz", [P, F, W])
        tr = sb("tr", [P, F, W])
        hv = sb("hv", [P, F, W])
        x1 = sb("x1", [P, GB, D])
        x1b = sb("x1b", [P, 2, GB, D])
        xnT = sb("xnT", [P, F, W])

        upad = sb("upad", [P, 2, 2, GB, TAPS - 1 + L])
        cv = sb("cv", [P, 2, 2, W])
        uth = sb("uth", [P, 2, W])
        zb = sb("zb", [P, 2, W])
        zth = sb("zth", [P, 2, W])
        u2 = sb("u2", [P, 2, C, W])
        sz2 = sb("sz2", [P, 2, C, W])
        delta = sb("delta", [P, 2, C, W])
        sp = sb("sp", [P, C, W])
        dt_sb = sb("dt_sb", [DR, W])
        rest = sb("rest", [2 * NS, W])
        mid = sb("mid", [2 * NS, W], BF16)
        split = sb("split", [96, W], BF16)
        bc = sb("bc", [P, 2, NS, W])

        du = sb("du", [P, 2, W])
        dbu = sb("dbu", [P, 2, Q, W])
        hc = sb("hc", [P, 2, Q, W])
        hs = sb("hs", [P, 2, Q, W])

        dA = ps("dA", [P, 2, Q, GB, L])
        yp = ps("yp", [P, 2, 2, W])
        gb = ps("gb", [P, 2, W])
        pb = ps("pb", [P, 2, W])

        win_raw = bc[:, :, :, :].rearrange("p a s w -> p (a s w)").rearrange("p (k e) -> p k e", k=M4)
        wout_raw = u2[:, :, :, :].rearrange("p a c w -> p (a c w)").rearrange("p (k e) -> p k e", k=M4)
        fc1_raw = dbu[:, 0, :, :]
        fc2_raw = dbu[:, 1, :, :]
        gate_raw = delta[:, :, :, :].rearrange("p a c w -> p (a c) w")

        s_load = sem("s_load")
        s_raw = sem("s_raw")
        s_const = sem("s_const")
        s_prep = sem("s_prep")
        s_fused = sem("s_fused")
        s_kept = sem("s_kept")
        s_alog = sem("s_alog")
        x_landed = [sem("x_landed0"), sem("x_landed1")]
        out_stored = sem("out_stored")
        stats_done = sem("stats_done")
        moments = sem("moments")
        aggregated = sem("aggregated")
        rstd_done = sem("rstd_done")
        normed = sem("normed")
        gnn_mm = sem("gnn_mm")
        gnn_read = sem("gnn_read")
        rh_done = sem("rh_done")
        diff_done = sem("diff_done")
        gated = sem("gated")
        h_new = sem("h_new")
        x1_saved = sem("x1_saved")
        proj_mm = sem("proj_mm")
        proj_read = sem("proj_read")
        conv_step = sem("conv_step")
        uth_done = sem("uth_done")
        u2_done = sem("u2_done")
        zth_done = sem("zth_done")
        sz_done = sem("sz_done")
        dt_done = sem("dt_done")
        hi_done = sem("hi_done")
        mid_done = sem("mid_done")
        split_done = sem("split_done")
        sp_min = sem("sp_min")
        sp_exp = sem("sp_exp")
        sp_ln = sem("sp_ln")
        delta_done = sem("delta_done")
        du_done = sem("du_done")
        dA_done = sem("dA_done")
        dA_free = sem("dA_free")
        dbu_done = sem("dbu_done")
        scanned = sem("scanned")
        hc_even = sem("hc_even")
        hc_odd = sem("hc_odd")
        summed = sem("summed")
        y_read = sem("y_read")
        y_gated = sem("y_gated")
        out_mm = sem("out_mm")
        out_added = sem("out_added")

        block = ctx.enter_context(nc.Block())

        GNN_LOADS = [
            (adj_sb[:, :], adjT), (par[:, :], cols),
            (gate_raw[:, 0:4, :], w3T.rearrange("(k p) n -> p k n", p=P)),
            (gate_raw[:, 4:8, :], w4T.rearrange("(k p) n -> p k n", p=P)),
            (gate_raw[:, 8:12, :], w5T.rearrange("(k p) n -> p k n", p=P)),
            (u3[:, :, :], u3T.rearrange("(k p) n -> p k n", p=P)),
            (u5h[:, :, :], u5T.rearrange("(k p) n -> p k n", p=P)),
            (bfc2_sb[:, :], bfc2.partition_broadcast(P)), (wdt[:, :], wdtT),
            (wx[:, :, :], wxT.rearrange("(k p) n -> p k n", p=P))]
        RAW_LOADS = [
            (fc1_raw, fc1.rearrange("(k p) n -> p k n", p=P)),
            (fc2_raw, fc2T.rearrange("(k p) n -> p k n", p=P)),
            (win_raw, winT.rearrange("(k p) n -> p k n", p=P)),
            (wout_raw, wout.rearrange("(k p) n -> p k n", p=P))]
        N_LOAD = 16 * len(GNN_LOADS)
        N_RAW = 16 * len(RAW_LOADS)
        N_CONST = 7
        N_PREP = 16
        N_WIN = F * (2 * DI // 512)
        N_WF = C // 2
        N_FUSED = N_WIN + N_WF + 1
        AT_FUSE = tuple(range(AT_T0, AT_T0 + 2 * N_FUSED, 2))

        def col(name, i=0, n=1):
            a = COLS[name][0] + i
            return par[:, a:a + n]

        x_v = x.rearrange("(g b) l d -> g l b d", b=GB)
        out_v = out.rearrange("(g b) l d -> g l b d", b=GB)

        @block.sync
        def _(sp_eng):
            for dst, src in GNN_LOADS:
                sp_eng.dma_start(dst, src).then_inc(s_load, 16)

            def body(gn, pr, sc, tl, fuse=False):
                if gn:
                    wait(sp_eng, gnn_read, GU * gn.n - 2 * GU + GU - 1)
                    sp_eng.dma_start(xin[:, gn.par, :, :], x_v[gn.n]).then_inc(x_landed[gn.par], 16)
                if fuse:
                    for dst, src in RAW_LOADS:
                        sp_eng.dma_start(dst, src).then_inc(s_raw, 16)
                if tl:
                    wait(sp_eng, out_added, GB * (tl.n + 1))
                    sp_eng.dma_start(out_v[tl.n], x1b[:, tl.par, :, :]).then_inc(out_stored, 16)

            bodies(sp_eng, body)
            sp_eng.wait_ge(out_stored, 16 * G)

        @block.tensor
        def _(pe):
            mm = nc.tensor.matmul
            pe.wait_ge(s_load, N_LOAD)
            pe.wait_ge(s_const, N_CONST)
            pe.wait_ge(s_prep, N_PREP - 2)

            def fused(use):
                pe.wait_ge(s_raw, N_RAW)
                wait(pe, s_kept, use)
                o = pb[:, :, :].rearrange("p a w -> p (a w)")
                if use < N_WIN:
                    f, n = divmod(use, 2 * DI // 512)
                    for k in range(M4):
                        last = mm(o, fc1_raw[:, k, f * P:(f + 1) * P], win_raw[:, k, n * 512:(n + 1) * 512],
                                  start=(k == 0), stop=(k == M4 - 1))
                elif use < N_WIN + N_WF:
                    for i in range(2):
                        c = 2 * (use - N_WIN) + i
                        for k in range(M4):
                            last = mm(o[:, i * D:(i + 1) * D], wout_raw[:, k, c * P:(c + 1) * P],
                                      fc2_raw[:, k, :], start=(i == 0 and k == 0), stop=(k == M4 - 1),
                                      skip_group_check=True)
                else:
                    for e in range(2 * C):
                        for k in range(M4):
                            last = mm(o[:, e:e + 1], win_raw[:, k, e * P:(e + 1) * P], col("bfc1", k),
                                      start=(e == 0 and k == 0), stop=(k == M4 - 1), skip_group_check=True)
                last.then_inc(s_fused, 1)

            def gates(pairs, first, final=True):
                for fo in range(F):
                    for i, (w, t) in enumerate(pairs):
                        for fi in range(F):
                            last = mm(gb[:, fo, :], w[:, fi, fo * P:(fo + 1) * P], t[:, fi, :],
                                      start=(first and fo == 0 and i == 0 and fi == 0),
                                      stop=(final and i == len(pairs) - 1 and fi == F - 1), skip_group_check=True)
                return last

            def gnn(g, n):
                def bank(use):
                    wait(pe, gnn_read, GU * g.n + use)

                if n == AT_T0:
                    pe.wait_ge(normed, 2 * g.n + 1)
                    bank(0)
                    for b in range(GB):
                        for f in range(F):
                            last = nc.tensor.transpose(gb[:, f, b * L:(b + 1) * L],
                                                       h_tok[:, b, f * P:(f + 1) * P], ident[:, :])
                    last.then_inc(gnn_mm, 1)
                k, at = divmod(n - AT_ROUND, ROUND_STEPS)
                if 0 <= k < ROUNDS:
                    if at == AT_A:
                        bank(1 + 5 * k)
                        for f in range(F):
                            for b in range(GB):
                                last = mm(gb[:, f, b * L:(b + 1) * L], h_tok[:, b, f * P:(f + 1) * P],
                                          adj_sb[:, :], start=True, stop=True, skip_group_check=True)
                        last.then_inc(gnn_mm, 1)
                    if at == AT_ZG[0]:
                        bank(2 + 5 * k)
                        gates([(w3s, a_sb)], True, False)
                    if at == AT_ZG[1]:
                        gates([(u3, hT)], False).then_inc(gnn_mm, 1)
                    if at == AT_RG:
                        bank(3 + 5 * k)
                        gates([(w43, a_sb)], False).then_inc(gnn_mm, 1)
                    if at == AT_HV[0]:
                        bank(4 + 5 * k)
                        gates([(w5s, a_sb)], True, False)
                    if at == AT_HV[1]:
                        pe.wait_ge(rh_done, ROUNDS * g.n + k + 1)
                        gates([(u5h, tr)], False).then_inc(gnn_mm, 1)
                    if at == AT_T:
                        bank(5 + 5 * k)
                        pe.wait_ge(h_new, ROUNDS * g.n + k + 1)
                        gt = gb[:, :, :].rearrange("p a w -> p (a w)")
                        for b in range(GB):
                            for f in range(F):
                                last = nc.tensor.transpose(gt[:, b * D + f * P:b * D + (f + 1) * P],
                                                           hT[:, f, b * L:(b + 1) * L], ident[:, :])
                        last.then_inc(gnn_mm, 1)

            def norm2_turned(g):
                pe.wait_ge(normed, 2 * g.n + 2)
                pe.wait_ge(gnn_read, GU * g.n + GU - 1)
                for b in range(GB):
                    for f in range(F):
                        last = nc.tensor.transpose(gb[:, f, b * L:(b + 1) * L],
                                                   h_tok[:, b, f * P:(f + 1) * P], ident[:, :])
                last.then_inc(gnn_mm, 1)

            def proj_bank(g, use):
                if isinstance(g.n, int) and g.n == 0 and use == 0:
                    pe.wait_ge(s_kept, N_FUSED)
                wait(pe, proj_read, PU * g.n + use)

            def proj(g, n):
                if n in AT_U or n in AT_Z:
                    if n == AT_U[0]:
                        pe.wait_ge(gnn_read, GU * g.n + GU)
                    proj_bank(g, PROJ_ORDER.index(n))
                    first = 2 * AT_U.index(n) if n in AT_U else C + 2 * AT_Z.index(n)
                    for i in range(2):
                        e = (first + i) * P
                        for f in range(F):
                            last = mm(pb[:, i, :], win[:, f, e:e + P], xnT[:, f, :],
                                      start=(i == 0 and f == 0), stop=(f == F - 1), skip_group_check=True)
                    last.then_inc(proj_mm, 1)
                if n in AT_X:
                    half = AT_X.index(n)
                    pe.wait_ge(u2_done, C // 2 * g.n + C // 4 * (half + 1))
                    if half == 0:
                        proj_bank(g, PU_X)
                    for c in range(half * C // 2, (half + 1) * C // 2):
                        last = mm(pb[0:2 * NS + DR, 0, :], wx[:, c, :], u2[:, g.par, c, :],
                                  start=(c == 0), stop=(c == C - 1))
                    if half:
                        last.then_inc(proj_mm, 1)
                if n in AT_DT:
                    pe.wait_ge(dt_done, g.n + 1)
                    p = AT_DT.index(n)
                    proj_bank(g, PU_DT[p])
                    for i in range(2):
                        c = 2 * p + i
                        last = mm(pb[:, i, :], wdt[:, c * P:(c + 1) * P], dt_sb[:, :],
                                  start=(i == 0), stop=True, skip_group_check=True)
                    last.then_inc(proj_mm, 1)

            def spread(g, first, row, q, r):
                proj_bank(g, first + Q // 2 * q + r)
                for i in range(2):
                    last = mm(pb[:, i, :], sel[:, row + Q * q + 2 * r + i, :], split[:, :],
                              start=(i == 0), stop=True, skip_group_check=True)
                last.then_inc(proj_mm, 1)

            def rows(sc, pr, n, r):
                if pr and AT_B <= n < AT_C:
                    if n == AT_B and r == 0:
                        pe.wait_ge(split_done, pr.n + 1)
                    spread(pr, PU_B, 0, n - AT_B, r)
                if pr and n == AT_C:
                    spread(pr, PU_C, NS, 0, r)
                if sc and n < NQ - 1:
                    spread(sc, PU_C, NS, n + 1, r)

            def state_sum(g, m):
                c, q = divmod(m, NQ)
                if q == 0:
                    wait(pe, y_read, C * g.n + c - 1)
                    if GB <= c < 2 * GB:
                        wait(pe, out_added, GB * g.n - 2 * GB + c + 1)
                src = hs if m % 2 else hc
                pe.wait_ge(hc_odd if m % 2 else hc_even, STEPS // 2 * g.n + m // 2 + 1)
                for s in range(Q):
                    last = mm(yp[:, c % 2, 0, :], ident[:, :], src[:, m // 2 % 2, s, :],
                              start=(q == 0 and s == 0), stop=(q == NQ - 1 and s == Q - 1))
                last.then_inc(summed, 1)

            def out_part(g, part, alone):
                b, c0 = divmod(part * GB * C // len(AT_OUT), C)
                if alone and c0 == 0 and b == 0:
                    pe.wait_ge(y_read, C * g.n + C - 1)
                if alone and c0 == 0 and b == 1:
                    pe.wait_ge(y_read, C * g.n + C)
                for c in range(c0, c0 + GB * C // len(AT_OUT)):
                    if b == 0:
                        pe.wait_ge(y_gated, C * g.n + c + 1)
                    last = mm(yp[:, b, 1, :], sz2[:, g.par, c, b * L:(b + 1) * L], wf[:, c, :],
                              start=(alone and c == 0), stop=(c == C - 1), skip_group_check=True)
                if c == C - 1:
                    last.then_inc(out_mm, 1)

            def body(gn, pr, sc, tl, fuse=False):
                for n in range(STEPS):
                    if n < 2 and tl:
                        state_sum(tl, STEPS - 2 + n)
                    if n >= 2 and sc:
                        state_sum(sc, n - 2)
                    rows(sc, pr, n, 0)
                    if pr and n == 0:
                        norm2_turned(pr)
                    if gn:
                        gnn(gn, n)
                    if fuse and n in AT_FUSE:
                        fused(AT_FUSE.index(n))
                    if pr:
                        proj(pr, n)
                    if tl and n in AT_OUT:
                        out_part(tl, AT_OUT.index(n), not sc)
                    rows(sc, pr, n, 1)

            bodies(pe, body)

        @block.scalar
        def _(act):
            fn = nc.scalar.activation
            act.wait_ge(s_load, N_LOAD)
            fn(col("alog", 0, C * NS), col("alog", 0, C * NS), ACT.Exp).then_inc(s_alog, 1)
            act.wait_ge(s_prep, N_PREP - 2)
            act.wait_ge(s_const, N_CONST)

            def fused_kept(use):
                act.wait_ge(s_fused, use + 1)
                if use < N_WIN:
                    f, n = divmod(use, 2 * DI // 512)
                    fn(win[:, f, n * 512:(n + 1) * 512], pb[:, :, :].rearrange("p a w -> p (a w)"), ACT.Copy)\
                        .then_inc(s_kept, 1)
                elif use < N_WIN + N_WF:
                    c = 2 * (use - N_WIN)
                    fn(wf[:, c:c + 2, :], pb[:, :, :], ACT.Copy, scale=0.25).then_inc(s_kept, 1)
                else:
                    fn(cu[:, :], pb[:, 0, 0:2 * C], ACT.Copy).then_inc(s_kept, 1)
                    act.wait_ge(s_prep, N_PREP)

            def gnn(g, n):
                def filled(use):
                    act.wait_ge(gnn_mm, GU * g.n + use + 1)

                def gate(dst, bias, scale):
                    for fo in range(F):
                        last = fn(dst[:, fo, :], gb[:, fo, :], ACT.Tanh, bias=bias[:, fo:fo + 1], scale=scale)
                    last.then_inc(gnn_read, 1)

                if n == AT_T0:
                    filled(0)
                    fn(hT[:, :, :], gb[:, :, :], ACT.Copy).then_inc(gnn_read, 1)
                k, at = divmod(n - AT_ROUND, ROUND_STEPS)
                if 0 <= k < ROUNDS:
                    if at == AT_A:
                        filled(1 + 5 * k)
                        fn(a_sb[:, :, :], gb[:, :, :], ACT.Copy).then_inc(gnn_read, 1)
                    if at == AT_ZG[1]:
                        filled(2 + 5 * k)
                        gate(tz, bz, 0.5)
                    if at == AT_RG:
                        filled(3 + 5 * k)
                        gate(tr, br, 0.5)
                    if at == AT_HV[1]:
                        filled(4 + 5 * k)
                        gate(hv, bv, 1.0)
                    if at == AT_T and k < ROUNDS - 1:
                        filled(5 + 5 * k)
                        fn(h_tok[:, :, :].rearrange("p b d -> p (b d)"),
                           gb[:, :, :].rearrange("p a w -> p (a w)"), ACT.Copy).then_inc(gnn_read, 1)

            def norm2_kept(g):
                act.wait_ge(gnn_mm, GU * g.n + GU)
                fn(xnT[:, :, :], gb[:, :, :], ACT.Copy).then_inc(gnn_read, 1)

            def filled(g, use):
                act.wait_ge(proj_mm, PU * g.n + use + 1)

            def proj(g, n):
                if n - 1 in AT_U:
                    p = AT_U.index(n - 1)
                    s = p % 2
                    wait(act, u2_done, C // 2 * g.n + p - 1)
                    filled(g, PU_U[p])
                    for i in range(2):
                        c = 2 * p + i
                        fn(upad[:, s, i, :, TAPS - 1:TAPS - 1 + L],
                           pb[:, i, :].rearrange("p (b l) -> p b l", b=GB), ACT.Identity, bias=cu[:, c:c + 1])
                        last = fn(cv[:, s, i, :], pb[:, i, :], ACT.Identity, bias=wcu[:, c:c + 1],
                                  scale=col("convw", c * TAPS + TAPS - 1))
                    last.then_inc(proj_read, 1)
                if n - 1 in AT_Z:
                    p = AT_Z.index(n - 1)
                    wait(act, sz_done, C // 2 * g.n + p)
                    filled(g, PU_Z[p])
                    for i in range(2):
                        c = 2 * p + i
                        last = fn(zb[:, i, :], pb[:, i, :], ACT.Identity, bias=cu[:, C + c:C + c + 1])
                    last.then_inc(proj_read, 1)
                    act.wait_ge(proj_read, PU * g.n + PU_Z[p] + 1)
                    fn(zth[:, :, :], zb[:, :, :], ACT.Tanh, scale=0.5).then_inc(zth_done, 1)
                if n - 3 in AT_U:
                    p = AT_U.index(n - 3)
                    act.wait_ge(conv_step, 3 * C * g.n + 6 * p + 6)
                    wait(act, u2_done, C // 2 * g.n + p)
                    fn(uth[:, :, :], cv[:, p % 2, :, :], ACT.Tanh, scale=0.5).then_inc(uth_done, 1)
                if n == AT_X[1] + 1:
                    filled(g, PU_X)
                    fn(dt_sb[:, :], pb[2 * NS:2 * NS + DR, 0, :], ACT.Copy).then_inc(dt_done, 1)
                    fn(split[0:2 * NS, :], pb[0:2 * NS, 0, :], ACT.Copy).then_inc(hi_done, 1)
                if n == AT_X[1] + 2:
                    act.wait_ge(proj_read, PU * g.n + PU_X + 1)
                    fn(split[2 * NS:4 * NS, :], rest[:, :], ACT.Copy)
                    fn(mid[:, :], rest[:, :], ACT.Copy).then_inc(mid_done, 1)
                if n - 1 in AT_DT:
                    p = AT_DT.index(n - 1)
                    filled(g, PU_DT[p])
                    for i in range(2):
                        c = 2 * p + i
                        last = fn(delta[:, g.par, c, :], pb[:, i, :], ACT.Identity, bias=col("bdt", c))
                    last.then_inc(proj_read, 1)
                if n == AT_EXP:
                    act.wait_ge(sp_min, g.n + 1)
                    fn(sp[:, :, :], sp[:, :, :], ACT.Exp).then_inc(sp_exp, 1)
                if n == AT_LN:
                    act.wait_ge(sp_exp, g.n + 1)
                    fn(sp[:, :, :], sp[:, :, :], ACT.Ln, bias=1.0).then_inc(sp_ln, 1)

            def rows(sc, pr, n, r):
                if pr and AT_B <= n < AT_C:
                    q = n - AT_B
                    if r == 0:
                        wait(act, dbu_done, STEPS * pr.n - NQ + q + 1)
                    keep(pr, PU_B, 0, q, r)
                if pr and n == AT_C:
                    c_rows(pr, 0, r)
                if sc and n < NQ - 1:
                    c_rows(sc, n + 1, r)

            def c_rows(g, q, r):
                if r == 0:
                    wait(act, hc_odd if q % 2 else hc_even, STEPS // 2 * g.n - NQ // 2 + q // 2 + 1)
                keep(g, PU_C, 1, q, r)

            def keep(g, first, which, q, r):
                filled(g, first + Q // 2 * q + r)
                s = Q * q + 2 * r
                fn(bc[:, which, s:s + 2, :], pb[:, :, :], ACT.Copy).then_inc(proj_read, 1)

            def decay(g, n):
                c, q = divmod(n, NQ)
                if n % (STEPS // 2) == 0:
                    act.wait_ge(delta_done, 2 * g.n + 2 * n // STEPS + 1)
                if n % 2:
                    wait(act, scanned, STEPS * g.n + n - 1)
                else:
                    wait(act, dA_free, STEPS // 2 * g.n + n // 2)
                src = delta[:, g.par, c, :].rearrange("p (b l) -> p b l", b=GB)[:, :, 1:L]
                for i in range(Q):
                    last = fn(dA[:, n % 2, i, :, 1:L], src, ACT.Exp, scale=col("alog", c * NS + Q * q + i))
                last.then_inc(dA_done, 1)

            def body(gn, pr, sc, tl, fuse=False):
                for n in range(STEPS):
                    if n:
                        rows(sc, pr, n - 1, 1)
                    elif sc:
                        c_rows(sc, 0, 1)
                    if sc and n < STEPS - 1:
                        decay(sc, n + 1)
                    if pr and n == STEPS - 1:
                        decay(pr, 0)
                    if pr and n == 1:
                        norm2_kept(pr)
                    if gn and n:
                        gnn(gn, n - 1)
                    if fuse and n - 1 in AT_FUSE:
                        fused_kept(AT_FUSE.index(n - 1))
                    if pr:
                        proj(pr, n)
                    rows(sc, pr, n, 0)

            bodies(act, body)

        @block.vector
        def _(dve):
            tt = nc.vector.tensor_tensor
            stt = nc.vector.scalar_tensor_tensor
            nc.vector.memset(dA[:, :, :, :, :].rearrange("p a s b l -> p (a s b) l")[:, :, 0:1], 0.0)\
                .then_inc(s_prep, 1)
            nc.vector.memset(upad[:, :, :, :, 0:TAPS - 1].rearrange("p a i b l -> p (a i b) l"), 0.0)\
                .then_inc(s_prep, 1)
            dve.wait_ge(s_load, N_LOAD)
            for i, w in enumerate((w3s, w43, w5s)):
                raw = gate_raw[:, 4 * i:4 * i + 4, :]
                tt(w[:, :, :], raw[:, 0:F, :], raw[:, F:2 * F, :], ALU.add).then_inc(s_prep, 1)
            dve.wait_ge(s_prep, 5)
            tt(w43[:, :, :], w43[:, :, :], w3s[:, :, :], ALU.subtract).then_inc(s_prep, 1)
            nc.vector.tensor_scalar(u5h[:, :, :], u5h[:, :, :], 0.5, None, ALU.mult).then_inc(s_prep, 1)
            nc.vector.tensor_scalar(wx[:, :, :], wx[:, :, :], 0.5, None, ALU.mult).then_inc(s_prep, 1)
            tt(bz[:, :], col("w3b", 0, F), col("u3b", 0, F), ALU.add).then_inc(s_prep, 1)
            tt(br[:, :], col("w4b", 0, F), col("u3b", 0, F), ALU.add).then_inc(s_prep, 1)
            tt(bv[:, :], col("w5b", 0, F), col("u5b", 0, F), ALU.add).then_inc(s_prep, 1)
            dve.wait_ge(s_prep, 11)
            nc.vector.tensor_scalar(bz[:, :], bz[:, :], 0.5, None, ALU.mult).then_inc(s_prep, 1)
            nc.vector.tensor_scalar(br[:, :], br[:, :], 0.5, None, ALU.mult).then_inc(s_prep, 1)
            dve.wait_ge(s_alog, 1)
            nc.vector.tensor_scalar(col("alog", 0, C * NS), col("alog", 0, C * NS), -1.0, None, ALU.mult)\
                .then_inc(s_prep, 1)
            dve.wait_ge(s_prep, N_PREP - 2)

            def last_tap_bias():
                dve.wait_ge(s_kept, N_FUSED)
                last_tap = col("convw", 0, C * TAPS).rearrange("p (c t) -> p c t", t=TAPS)[:, :, TAPS - 1]
                tt(wcu[:, :], last_tap, cu[:, 0:C], ALU.mult).then_inc(s_prep, 1)
                dve.wait_ge(s_prep, N_PREP - 1)
                tt(wcu[:, :], wcu[:, :], col("convb", 0, C), ALU.add).then_inc(s_prep, 1)

            def norm_stats(src, done):
                for b in range(GB):
                    last = nc.vector.bn_stats(stats[:, b, :], src[:, b, :])
                last.then_inc(stats_done, 1)
                dve.wait_ge(stats_done, done)
                nc.vector.memset(ve[:, :], 0.0)
                for b in range(GB):
                    last = nc.vector.bn_aggr(mv[:, b, :], stats[:, b, :])
                last.then_inc(aggregated, 1)
                dve.wait_ge(aggregated, done)
                nc.vector.tensor_scalar(ve[:, :], mv[:, :, 1], EPS, None, ALU.add).then_inc(moments, 1)

            def normalise(dst, src):
                for b in range(GB):
                    last = nc.vector.tensor_scalar(dst[:, b, :], src[:, b, :], mv[:, b, 0:1], rstd[:, b:b + 1],
                                                   ALU.subtract, ALU.mult)
                last.then_inc(normed, 1)

            def gnn(g, n):
                if n == 0:
                    dve.wait_ge(x_landed[g.par], 16 * g.half + 16)
                    norm_stats(xin[:, g.par, :, :], 2 * g.n + 1)
                if n == AT_T0:
                    dve.wait_ge(rstd_done, 2 * g.n + 1)
                    wait(dve, gnn_read, GU * g.n)
                    normalise(h_tok, xin[:, g.par, :, :])
                k, at = divmod(n - AT_ROUND, ROUND_STEPS)
                if 0 <= k < ROUNDS:
                    if at == AT_RH:
                        dve.wait_ge(gnn_read, GU * g.n + 4 + 5 * k)
                        stt(tr[:, :, :], tr[:, :, :], 1.0, hT[:, :, :], ALU.add, ALU.mult).then_inc(rh_done, 1)
                    if at == AT_T:
                        dve.wait_ge(diff_done, ROUNDS * g.n + k + 1)
                        stt(hv[:, :, :], tz[:, :, :], 1.0, hv[:, :, :], ALU.add, ALU.mult).then_inc(gated, 1)
                        dve.wait_ge(gated, ROUNDS * g.n + k + 1)
                        stt(hT[:, :, :], hv[:, :, :], 0.5, hT[:, :, :], ALU.mult, ALU.add).then_inc(h_new, 1)
                if n == AT_X1:
                    dve.wait_ge(gnn_mm, GU * g.n + GU - 1)
                    wait(dve, x1_saved, g.n)
                    tt(x1[:, :, :].rearrange("p b d -> p (b d)"), gb[:, :, :].rearrange("p a w -> p (a w)"),
                       xin[:, g.par, :, :].rearrange("p b d -> p (b d)"), ALU.add).then_inc(gnn_read, 1)
                    dve.wait_ge(gnn_read, GU * g.n + GU - 1)
                    norm_stats(x1, 2 * g.n + 2)

            def proj(g, n):
                if n - 2 in AT_U:
                    p = AT_U.index(n - 2)
                    s = p % 2
                    dve.wait_ge(proj_read, PU * g.n + PU_U[p] + 1)
                    for k in range(TAPS - 1):
                        for i in range(2):
                            c = 2 * p + i
                            if k:
                                dve.wait_ge(conv_step, 3 * C * g.n + 6 * p + 2 * k - 1 + i)
                            acc = cv[:, s, i, :].rearrange("p (b l) -> p b l", b=GB)
                            stt(acc, upad[:, s, i, :, k:k + L], col("convw", c * TAPS + k), acc,
                                ALU.mult, ALU.add).then_inc(conv_step, 1)
                if n - 2 in AT_Z:
                    p = AT_Z.index(n - 2)
                    dve.wait_ge(zth_done, C // 2 * g.n + p + 1)
                    if p == 0:
                        wait(dve, out_mm, GB * (g.n - 1))
                    stt(sz2[:, g.par, 2 * p:2 * p + 2, :], zth[:, :, :], 1.0, zb[:, :, :], ALU.add, ALU.mult)\
                        .then_inc(sz_done, 1)
                if n - 4 in AT_U:
                    p = AT_U.index(n - 4)
                    dve.wait_ge(uth_done, C // 2 * g.n + p + 1)
                    stt(u2[:, g.par, 2 * p:2 * p + 2, :], uth[:, :, :], 1.0, cv[:, p % 2, :, :],
                        ALU.add, ALU.mult).then_inc(u2_done, 1)
                if n == AT_X[1] + 2:
                    dve.wait_ge(hi_done, g.n + 1)
                    tt(rest[:, :], pb[0:2 * NS, 0, :], split[0:2 * NS, :], ALU.subtract).then_inc(proj_read, 1)
                if n == AT_X[1] + 3:
                    dve.wait_ge(mid_done, g.n + 1)
                    tt(split[4 * NS:6 * NS, :], rest[:, :], mid[:, :], ALU.subtract).then_inc(split_done, 1)
                if n == AT_MIN:
                    dve.wait_ge(proj_read, PU * g.n + PU_DT[-1] + 1)
                    nc.vector.tensor_scalar(sp[:, :, :], delta[:, g.par, :, :], CAP, None, ALU.min)\
                        .then_inc(sp_min, 1)
                if n in AT_MAX:
                    half = AT_MAX.index(n)
                    dve.wait_ge(sp_ln, g.n + 1)
                    cs = slice(half * C // 2, (half + 1) * C // 2)
                    tt(delta[:, g.par, cs, :], delta[:, g.par, cs, :], sp[:, cs, :], ALU.max)\
                        .then_inc(delta_done, 1)
                if n == AT_DU0:
                    dve.wait_ge(delta_done, 2 * g.n + 1)
                    wait(dve, dbu_done, STEPS * g.n - NQ)
                    input_scale(g, 0)

            def input_scale(g, c):
                tt(du[:, c % 2, :], delta[:, g.par, c, :], u2[:, g.par, c, :], ALU.mult).then_inc(du_done, 1)

            def scan(g, n):
                dve.wait_ge(dA_done, STEPS * g.n + n + 1)
                dve.wait_ge(dbu_done, STEPS * g.n + n + 1)
                a = dA[:, n % 2, :, :, :].rearrange("p s b l -> p (s b l)")
                if n % 2:
                    wait(dve, summed, STEPS * g.n + n - 3)
                    dst = hs[:, n // 2 % 2, :, :].rearrange("p s w -> p (s w)")
                else:
                    dst = a
                nc.vector.tensor_tensor_scan(dst, a, dbu[:, n % 2, :, :].rearrange("p s w -> p (s w)"),
                                             0.0, ALU.mult, ALU.add).then_inc(scanned, 1)

            def times_c(g, n):
                c, q = divmod(n, NQ)
                dve.wait_ge(scanned, STEPS * g.n + n + 1)
                if c == 0:
                    dve.wait_ge(proj_read, PU * g.n + PU_C + Q // 2 * (q + 1))
                wait(dve, summed, STEPS * g.n + n - 3)
                tt(hc[:, n // 2 % 2, :, :].rearrange("p s w -> p (s w)"),
                   dA[:, 0, :, :, :].rearrange("p s b l -> p (s b l)"),
                   bc[:, 1, Q * q:Q * q + Q, :].rearrange("p s w -> p (s w)"), ALU.mult).then_inc(hc_even, 1)

            def first_zeros(g, n):
                dve.wait_ge(hc_even, STEPS // 2 * g.n + n // 2 + 1)
                nc.vector.memset(dA[:, 0, :, :, :].rearrange("p s b l -> p (s b) l")[:, :, 0:1], 0.0)\
                    .then_inc(dA_free, 1)

            def gate_y(g, c):
                dve.wait_ge(summed, STEPS * g.n + NQ * (c + 1))
                if c < GB:
                    wait(dve, out_mm, GB * g.n - GB + c + 1)
                y = u2[:, g.par, c, :]
                stt(y, y, col("dskip", c), yp[:, c % 2, 0, :], ALU.mult, ALU.add)\
                    .then_inc(y_read, 1)
                dve.wait_ge(y_read, C * g.n + c + 1)
                tt(sz2[:, g.par, c, :], y, sz2[:, g.par, c, :], ALU.mult).then_inc(y_gated, 1)

            def body(gn, pr, sc, tl, fuse=False):
                for n in range(STEPS):
                    if sc:
                        scan(sc, n)
                    if pr and n == 0:
                        dve.wait_ge(rstd_done, 2 * pr.n + 2)
                        normalise(h_tok, x1)
                    if gn:
                        gnn(gn, n)
                    if fuse and n == AT_FUSE[-1] + 1:
                        last_tap_bias()
                    if sc and n % 2 == 0:
                        times_c(sc, n)
                        first_zeros(sc, n)
                    if sc and n % NQ == 1 and n // NQ < C - 1:
                        c = n // NQ + 1
                        if c == C // 2:
                            dve.wait_ge(delta_done, 2 * sc.n + 2)
                        if c >= 2:
                            dve.wait_ge(dbu_done, STEPS * sc.n + NQ * (c - 1))
                        input_scale(sc, c)
                    if sc and n >= NQ + 3 and n % NQ == 3:
                        gate_y(sc, n // NQ - 1)
                    if tl and n == AT_GATE7:
                        gate_y(tl, C - 1)
                    if tl and n in AT_ADD:
                        b = AT_ADD.index(n)
                        dve.wait_ge(out_mm, GB * tl.n + b + 1)
                        dve.wait_ge(x1_saved, tl.n + 1)
                        res = x1b[:, tl.par, b, :]
                        tt(res, yp[:, b, 1, :], res, ALU.add).then_inc(out_added, 1)
                    if pr:
                        proj(pr, n)

            bodies(dve, body)

        @block.gpsimd
        def _(pool):
            tt = nc.gpsimd.tensor_tensor
            nc.gpsimd.memset(ident[:, :], 0.0).then_inc(s_const, 1)
            nc.gpsimd.memset(sel[:, :, :], 0.0).then_inc(s_const, 1)
            nc.gpsimd.memset(mhalf[:, :], -0.5).then_inc(s_const, 1)
            pool.wait_ge(s_const, 3)
            nc.gpsimd.affine_select(out=ident[:, :], in_=ident[:, :], compare_op=ALU.not_equal, fill=1.0,
                                    base=0, pattern=[[-1, P]], channel_multiplier=1).then_inc(s_const, 1)
            for part in range(3):
                nc.gpsimd.affine_select(out=sel[:, :, :], in_=sel[:, :, :], compare_op=ALU.not_equal, fill=1.0,
                                        base=-2 * NS * part, pattern=[[-1, 2 * NS], [0, P]],
                                        channel_multiplier=1).then_inc(s_const, 1)
                pool.wait_ge(s_const, 5 + part)
            pool.wait_ge(s_load, N_LOAD)
            pool.wait_ge(s_prep, N_PREP - 2)

            def rstd_of(done):
                pool.wait_ge(moments, done)
                tt(rstd[:, :], ve[:, :], mhalf[:, :], ALU.pow).then_inc(rstd_done, 1)

            def gnn(g, n):
                if n == 1:
                    rstd_of(2 * g.n + 1)
                k, at = divmod(n - AT_ROUND, ROUND_STEPS)
                if 0 <= k < ROUNDS and at == AT_DIFF:
                    pool.wait_ge(gnn_read, GU * g.n + 5 + 5 * k)
                    tt(hv[:, :, :], hv[:, :, :], hT[:, :, :], ALU.subtract).then_inc(diff_done, 1)
                if n == AT_X1 + 1:
                    rstd_of(2 * g.n + 2)

            def input_rows(g, n):
                c, q = divmod(n, NQ)
                if q == 0:
                    pool.wait_ge(du_done, C * g.n + c + 1)
                if c == 0:
                    pool.wait_ge(proj_read, PU * g.n + PU_B + Q // 2 * (q + 1))
                wait(pool, scanned, STEPS * g.n + n - 1)
                tt(dbu[:, n % 2, :, :], du[:, c % 2, :].unsqueeze(1).to_broadcast([P, Q, W]),
                   bc[:, 0, Q * q:Q * q + Q, :], ALU.mult).then_inc(dbu_done, 1)

            def times_c(g, n):
                c, q = divmod(n, NQ)
                pool.wait_ge(scanned, STEPS * g.n + n + 1)
                if c == 0:
                    pool.wait_ge(proj_read, PU * g.n + PU_C + Q // 2 * (q + 1))
                h = hs[:, n // 2 % 2, :, :]
                tt(h, h, bc[:, 1, Q * q:Q * q + Q, :], ALU.mult).then_inc(hc_odd, 1)

            def body(gn, pr, sc, tl, fuse=False):
                for n in range(STEPS):
                    if sc and n < STEPS - 1:
                        input_rows(sc, n + 1)
                    if pr and n == STEPS - 1:
                        input_rows(pr, 0)
                    if tl and n == 0:
                        times_c(tl, STEPS - 1)
                    if sc and n and n % 2 == 0:
                        times_c(sc, n - 1)
                    if gn:
                        gnn(gn, n)
                    if pr and n == AT_SAVE:
                        pool.wait_ge(gnn_read, GU * pr.n + GU - 1)
                        wait(pool, out_stored, 16 * pr.n - 16)
                        tt(x1b[:, pr.par, :, :], x1[:, :, :],
                           bfc2_sb[:, :].unsqueeze(1).to_broadcast([P, GB, D]), ALU.add).then_inc(x1_saved, 1)

            bodies(pool, body)


def kernel(**inputs):
    import numpy as np
    import concourse.bacc as bacc
    from concourse.bass_utils import run_bass_kernel_spmd

    def get(name):
        return np.asarray(inputs[name])

    def column(v):
        v = v.reshape(v.shape[0] // P, P, -1)
        return v.transpose(1, 0, 2).reshape(P, -1)

    f = "L0_ffn_"
    n = "L0_gnn_"
    cols = np.concatenate([column(get(k)) for k in (
        n + "w3_b", n + "u3_b", n + "w4_b", n + "w5_b", n + "u5_b", f + "b_fc1", f + "conv_w",
        f + "conv_b", f + "b_dt", f + "A_log", f + "D")], axis=1)
    wxp = get(f + "W_xproj")
    arrays = {
        "x": get("x"), "adjT": get("adj").T,
        "w3T": get(n + "w3_w").T, "w4T": get(n + "w4_w").T, "w5T": get(n + "w5_w").T,
        "u3T": get(n + "u3_w").T, "u5T": get(n + "u5_w").T,
        "fc1": get(f + "W_fc1"), "winT": get(f + "W_in").T,
        "wxT": np.concatenate([wxp[DR:], wxp[:DR]], axis=0).T, "wdtT": get(f + "W_dt").T,
        "wout": get(f + "W_out"), "fc2T": get(f + "W_fc2").T, "bfc2": get(f + "b_fc2"), "cols": cols,
    }
    arrays = {k: np.ascontiguousarray(v) for k, v in arrays.items()}
    nc = bacc.Bacc("TRN2", target_bir_lowering=False, num_devices=1)
    args = [nc.dram_tensor(f"in_{k}", v.shape, mybir.dt.from_np(v.dtype), kind="ExternalInput").ap()
            for k, v in arrays.items()]
    args.append(nc.dram_tensor("out_0", (B, L, D), F32, kind="ExternalOutput").ap())
    build(nc, *args)
    r = run_bass_kernel_spmd(nc, [{f"in_{k}": v for k, v in arrays.items()}], core_ids=[0])
    return r.results[0]["out_0"]
```
